# Optimizing a Trainium2 kernel written in Bass

```python
import numpy as np
import jax
import jax.numpy as jnp

def _softmax(x, axis=-1):
    return jax.nn.softmax(x, axis=axis)

def _gelu(x):
    return jax.nn.gelu(x, approximate=True)

def _silu(x):
    return jax.nn.silu(x)

def _sigmoid(x):
    return jax.nn.sigmoid(x)

def _layernorm(x, axis=-1, eps=1e-05):
    m = jnp.mean(x, axis=axis, keepdims=True)
    v = jnp.var(x, axis=axis, keepdims=True)
    return (x - m) / jnp.sqrt(v + eps)

def _scatter_add(tgt, idx, src, axis=0):
    return tgt.at[idx].add(src)

def _segment_sum(src, seg, n):
    return jax.ops.segment_sum(src, seg, n)
kernel_name = 'mk_gnn_resnorm_d1_gnn_r64_321fbf'

def setup_inputs(seed: int=0):
    np.random.seed(seed)
    _w = jnp.asarray

    def _rec_inputs():
        import jax
        import jax.numpy as jnp
        _gk = jax.random.key(seed)
        x = -0.000202 + 1 * jax.random.normal(jax.random.fold_in(_gk, 1), (100000, 256), jnp.float32)
        src = jax.random.randint(jax.random.fold_in(_gk, 2), (25000,), 0, 100000, jnp.int32)
        dst = jnp.minimum((100000 * jax.random.uniform(jax.random.fold_in(_gk, 3), (25000,)) ** 2.0).astype(jnp.int32), 99999)
        _o = jnp.argsort(dst, stable=True)
        src = src[_o]
        dst = dst[_o]
        return (x, src, dst)
    x, src, dst = _rec_inputs()

    def _L0_gnn_setup():
        import jax, jax.numpy as jnp
        import numpy as np
        N_NODES = 25000
        N_EDGES = 6250
        D = 256
        key = jax.random.key(seed)
        k1, k2, k3, k4, k5 = jax.random.split(key, 5)
        feat = jax.random.normal(k1, (N_NODES, D), dtype=jnp.float32)
        src = jax.random.randint(k2, (N_EDGES,), 0, N_NODES, dtype=jnp.int32)
        dst = jax.random.randint(k3, (N_EDGES,), 0, N_NODES, dtype=jnp.int32)
        a = float(np.sqrt(6.0 / (D + D)))
        W1 = jax.random.uniform(k4, (D, D), minval=-a, maxval=a, dtype=jnp.float32)
        W2 = jax.random.uniform(k5, (D, D), minval=-a, maxval=a, dtype=jnp.float32)
        b = jnp.zeros((D,), dtype=jnp.float32)
        return {'feat': feat, 'W1': W1, 'W2': W2, 'b': b, 'src': src, 'dst': dst}
    _L0_gnn_all = _L0_gnn_setup()
    _L0_gnn_in = {k: v for k, v in _L0_gnn_all.items() if k in ('W1', 'W2', 'b')}
    del _L0_gnn_all
    return {'x': x, 'src': src, 'dst': dst, 'L0_gnn_W1': _L0_gnn_in['W1'], 'L0_gnn_W2': _L0_gnn_in['W2'], 'L0_gnn_b': _L0_gnn_in['b']}

def reference(x, src, dst, L0_gnn_W1, L0_gnn_W2, L0_gnn_b):
    import jax
    import jax.numpy as jnp

    def _L0_gnn_ref(feat, W1, W2, b, src, dst):
        import jax, jax.numpy as jnp
        import numpy as np
        N_NODES = 25000
        N_EDGES = 6250
        D = 256
        n = feat.shape[0]
        ones = jnp.ones(src.shape[0], dtype=feat.dtype)
        out_deg = jnp.maximum(jax.ops.segment_sum(ones, src, num_segments=n), 1.0)
        in_cnt = jax.ops.segment_sum(ones, dst, num_segments=n)
        t1 = feat @ W1
        msg = t1[src] + feat[src] * feat[dst] @ W2
        scale = jnp.sqrt(out_deg[src]) * jnp.sqrt(out_deg[dst])
        msg = msg / scale[:, None]
        agg = jax.ops.segment_sum(msg, dst, num_segments=n)
        embed = jnp.where(in_cnt[:, None] > 0, t1 + agg, jnp.zeros_like(t1))
        embed = embed + b
        embed = jax.nn.leaky_relu(embed, negative_slope=0.01)
        norm = jnp.linalg.norm(embed, axis=1, keepdims=True)
        embed = embed / jnp.maximum(norm, 1e-12)
        return embed
    x = _layernorm(x + _L0_gnn_ref(x, L0_gnn_W1, L0_gnn_W2, L0_gnn_b, src, dst), axis=-1)
    return x

_drawn_inputs = setup_inputs


def setup_inputs(seed=0):
    import zlib

    import numpy as np

    out = dict(_drawn_inputs(seed))
    spreads = {'L0_gnn_b': (0.0, 0.1)}
    factors = {}
    for name, (base, spread) in spreads.items():
        noise = np.random.default_rng([zlib.crc32(name.encode()), seed]).standard_normal(out[name].shape)
        drawn = base * np.exp(spread * noise) if base else spread * noise
        out[name] = jnp.asarray(drawn.astype(out[name].dtype))
    for name, factor in factors.items():
        out[name] = (out[name] * factor).astype(out[name].dtype)
    return out
```

```python
def gnn_resnorm(nc, x, src, dst, w1, w2, b, out):
    from contextlib import ExitStack

    import concourse.bass as bass
    from concourse import mybir

    F32, F16, I32 = mybir.dt.float32, mybir.dt.float16, mybir.dt.int32
    ALU = mybir.AluOpType
    ACT = mybir.ActivationFunctionType
    P = 128

    N, D = x.shape
    E = src.shape[0]
    KB = D // P
    TILES = -(-E // P)
    TOP = P
    REST = TILES - TOP
    E_LAST = E - (TILES - 1) * P
    HI = -(-N // P)
    HH = HI // 2
    TABLE = P * HI
    PAD_SRC = TABLE - 1
    PAD_DST = 150000
    SKIP = 1 << 18
    LN_EPS = 1e-5
    SLOPE = 0.01

    R = 8
    ROWS = P * R
    CHUNKS = N // ROWS
    LEFT = N - CHUNKS * ROWS
    RL = 7
    PL = LEFT // RL
    STEPS = CHUNKS + 1
    NX = 6
    D0 = 3
    DPASSES = (CHUNKS - D0) // NX
    D1 = D0 + DPASSES * NX
    LK = TILES // STEPS
    assert HI == 2 * HH and PL * RL == LEFT and LK * STEPS == TILES

    ER = 8
    EPASSES = TILES // ER - 1
    E0 = 4
    E1 = E0 + ER * EPASSES
    G0 = ER
    G1 = G0 + ER * EPASSES
    AHEAD = 4
    SCATTER_LAG = 8

    x_chunks = x[0:CHUNKS * ROWS, :].rearrange("(c p r) d -> c p (r d)", p=P, r=R)
    o_chunks = out[0:CHUNKS * ROWS, :].rearrange("(c p r) d -> c p (r d)", p=P, r=R)
    x_left = x[CHUNKS * ROWS:N, :].rearrange("(p r) d -> p (r d)", r=RL)
    o_left = out[CHUNKS * ROWS:N, :].rearrange("(p r) d -> p (r d)", r=RL)

    table = nc.dram_tensor("degree_root_table", (TABLE, 1), F32).ap()
    keys = nc.dram_tensor("edge_keys", (1 + TILES * P,), F32).ap()

    ctx = ExitStack()
    with ctx:
        def sb(name, shape, dt=F32):
            return ctx.enter_context(nc.sbuf_tensor(name, shape, dt))

        def pb(name, shape, dt=F32):
            return ctx.enter_context(nc.psum_tensor(name, shape, dt))

        def sem(name):
            return ctx.enter_context(nc.semaphore(name))

        def sems(name, n):
            return [sem(f"{name}{k}") for k in range(n)]

        ident = sb("ident", [P, P])
        iota_i = sb("iota_i", [P, HI], I32)
        iota_h = sb("iota_h", [P, HI], F16)
        w_sb = sb("w_sb", [P, 2, KB, D])
        brow = sb("brow", [1, D])
        ones = sb("ones", [1, P])
        eps = sb("eps", [P, 1])
        minus1 = sb("minus1", [1, 1])
        cst = sb("cst", [P, 1, D])
        bb = sb("bb", [P, D])
        cjunk = sb("cjunk", [P, D])
        cn = sb("cn", [P, 4])

        rows_i = sb("rows_i", [P, 3, 2, P], I32)
        rows_f = sb("rows_f", [P, 3, 2, P])
        cols = sb("cols", [P, 3, TILES])
        cols_i = sb("cols_i", [P, 2, TILES], I32)
        hilo_i = sb("hilo_i", [P, 2, 2, TILES], I32)
        hilo = sb("hilo", [P, 2, 2, TILES])
        tix_f = sb("tix_f", [P, TILES, 2])
        tix = sb("tix", [P, TILES, 2], I32)
        same = sb("same", [P, TILES])
        rix_f = sb("rix_f", [P, TILES, 2])
        rix = sb("rix", [P, TILES, 2], I32)
        weight = sb("weight", [P, TILES])

        oh_lo = sb("oh_lo", [P, 2, P], F16)
        oh_hi = sb("oh_hi", [P, 2, HI], F16)
        root = sb("root", [P, HI])

        xy = sb("xy", [P, NX, R, D])
        bst = sb("bst", [P, 2, R, 6])
        mv = sb("mv", [P, NX, R, 2])
        std = sb("std", [P, NX, R])
        rstd = sb("rstd", [P, NX, R])
        nmr = sb("nmr", [P, NX, R])
        lk_ix = sb("lk_ix", [P, 2, LK, 2], I32)
        lk_v = sb("lk_v", [P, 2, LK, 2])
        lk_p = sb("lk_p", [P, LK])

        xs = sb("xs", [P, ER, D])
        xd = sb("xd", [P, ER, D])
        gix = sb("gix", [P, ER, 2], I32)
        six = sb("six", [P, 4, 1], I32)
        kr = sb("kr", [P, 4, 1 + P])
        match = sb("match", [P, 2, P])
        goes_on = sb("goes_on", [P, 2, P])
        tsum = sb("tsum", [P, 2, KB, P])
        ab = sb("ab", [P, 2, 2, KB, P])
        z = sb("z", [P, 4, D])
        lr = sb("lr", [P, 4, D])
        sq = sb("sq", [P, 2, D])
        ss = sb("ss", [P, 4, 2])
        nr = sb("nr", [P, 4, 2])
        y = sb("y", [P, 4, D])
        est = sb("est", [P, 4, 6])
        emv = sb("emv", [P, 4, 2])
        esd = sb("esd", [P, 4, 2])
        eo = sb("eo", [P, 4, D])

        hist = [pb(f"hist{k}", [P, 512]) for k in range(2)]
        ps_t = [pb(f"ps_t{k}", [P, 512]) for k in range(2)]
        ps_x = [pb(f"ps_x{k}", [P, 512]) for k in range(2)]
        ps_e = [pb(f"ps_e{k}", [P, 512]) for k in range(2)]

        s_zero = sem("s_zero")
        s_ident = sem("s_ident")
        s_iota = sem("s_iota")
        s_go = sem("s_go")
        s_rows = sem("s_rows")
        s_bias = sem("s_bias")
        s_w = sem("s_w")
        s_setup = sem("s_setup")
        s_rows_f = sem("s_rows_f")
        s_keys = sem("s_keys")
        s_cols = sem("s_cols")
        s_cols_read = sem("s_cols_read")
        s_csq = sem("s_csq")
        s_cready = sem("s_cready")
        s_onehot = sem("s_onehot")
        s_hist = sem("s_hist")
        s_clip = sem("s_clip")
        s_root = sem("s_root")
        s_table = sem("s_table")
        s_load = sems("s_load", NX)
        s_store = sems("s_store", NX)
        s_added = sem("s_added")
        s_bst = sem("s_bst")
        s_var = sem("s_var")
        s_std = sem("s_std")
        s_recip = sem("s_recip")
        s_rstd = sem("s_rstd")
        s_normed = sem("s_normed")
        s_lkix = sem("s_lkix")
        s_lk = sems("s_lk", 2)
        s_lkp = sem("s_lkp")
        s_weight = sem("s_weight")
        s_gix = sem("s_gix")
        s_rowsin = sems("s_rowsin", ER)
        s_kr = sems("s_kr", 4)
        s_match = sem("s_match")
        s_tt = sem("s_tt")
        s_xt = sem("s_xt")
        s_tsum = sem("s_tsum")
        s_ab = sem("s_ab")
        s_emb = sem("s_emb")
        s_z = sem("s_z")
        s_leaky = sem("s_leaky")
        s_sq = sem("s_sq")
        s_norm = sem("s_norm")
        s_clamp = sem("s_clamp")
        s_unit = sem("s_unit")
        s_y = sem("s_y")
        s_est = sem("s_est")
        s_evar = sem("s_evar")
        s_esd = sem("s_esd")
        s_ers = sem("s_ers")
        s_eo = sem("s_eo")
        s_scat = sems("s_scat", 4)

        block = ctx.enter_context(nc.Block())

        def lap(n, k, i, off):
            return (n // k) * i + off // k

        def parts(c):
            return (PL, RL) if isinstance(c, int) and c == CHUNKS else (P, R)

        @block.sync
        def _(sp):
            def load(i, off):
                c, slot = NX * i + off, off % NX
                pc, rc = parts(c)
                if off >= NX or not isinstance(i, int):
                    sp.wait_ge(s_store[slot], 16 * lap(NX, NX, i, off))
                sp.dma_start(xy[0:pc, slot, 0:rc, :].rearrange("p r d -> p (r d)"),
                             x_left if pc == PL else x_chunks[c]).then_inc(s_load[slot], 16)

            def store(i, off):
                c, slot = NX * i + off, off % NX
                pc, rc = parts(c)
                sp.wait_ge(s_normed, c + 1)
                sp.dma_start(o_left if pc == PL else o_chunks[c],
                             xy[0:pc, slot, 0:rc, :].rearrange("p r d -> p (r d)")).then_inc(s_store[slot], 16)

            def load_keys(i, off):
                t = ER * i + off
                if off >= 4 or not isinstance(i, int):
                    sp.wait_ge(s_match, t - 3)
                sp.dma_start(kr[:, off % 4, :],
                             keys[bass.ds(t * P, 1 + P)].rearrange("(o e) -> o e", o=1).to_broadcast([P, 1 + P])
                             ).then_inc(s_kr[off % 4], 16)

            sp.wait_ge(s_zero, 1)
            for k, (vec, first) in enumerate(((src, 0), (dst, 0), (dst, 1))):
                full = (TILES - 1) * P
                sp.dma_start(rows_i[:, k, 0, :], vec[first:first + TOP * P].rearrange("(t e) -> t e", e=P)).then_inc(s_rows, 16)
                sp.dma_start(rows_i[0:REST - 1, k, 1, :],
                             vec[first + TOP * P:first + full].rearrange("(t e) -> t e", e=P)).then_inc(s_rows, 16)
                sp.dma_start(rows_i[REST - 1:REST, k, 1, 0:E_LAST - first],
                             vec[first + full:E].rearrange("(o e) -> o e", o=1)).then_inc(s_rows, 16)
            sp.dma_start(bb[:, :], b.rearrange("(o d) -> o d", o=1).to_broadcast([P, D])).then_inc(s_bias, 16)
            for c in range(3):
                load(0, c)
            sp.dma_start(brow[:, :], b.rearrange("(o d) -> o d", o=1)).then_inc(s_w, 16)
            sp.dma_start(w_sb[:, 0, :, :], w1.rearrange("(k p) n -> p k n", p=P)).then_inc(s_w, 16)
            sp.dma_start(w_sb[:, 1, :, :], w2.rearrange("(k p) n -> p k n", p=P)).then_inc(s_w, 16)
            sp.wait_ge(s_rows_f, 1)
            sp.dma_start(keys[0:1].rearrange("(o e) -> o e", o=1), minus1[:, :]).then_inc(s_keys, 16)
            sp.dma_start(keys[1:1 + TOP * P].rearrange("(t e) -> t e", e=P), rows_f[:, 1, 0, :]).then_inc(s_keys, 16)
            sp.dma_start(keys[1 + TOP * P:1 + TILES * P].rearrange("(t e) -> t e", e=P),
                         rows_f[0:REST, 1, 1, :]).then_inc(s_keys, 16)
            sp.wait_ge(s_root, 1)
            sp.dma_start(table.rearrange("(l h) o -> l (h o)", h=HI), root[:, :]).then_inc(s_table, 16)

            for c in range(D0):
                load(0, c + 3)
                if c >= 1:
                    store(0, c - 1)
            with sp.Fori(0, DPASSES) as i:
                for u in range(NX):
                    load(i, D0 + u + 3)
                    store(i, D0 + u - 1)
            for c in range(D1, STEPS + 1):
                if c + 3 < STEPS:
                    load(0, c + 3)
                store(0, c - 1)

            sp.wait_ge(s_keys, 48)
            for t in range(E0):
                load_keys(0, t)
            with sp.Fori(0, EPASSES) as i:
                for u in range(ER):
                    load_keys(i, E0 + u)
            for t in range(E1, TILES):
                load_keys(0, t)

        @block.gpsimd
        def _(pool):
            nc.gpsimd.memset(rows_i[:, 0, :, :], PAD_SRC)
            nc.gpsimd.memset(rows_i[:, 1, :, :], PAD_DST)
            nc.gpsimd.memset(rows_i[:, 2, :, :], PAD_DST + 1)
            nc.gpsimd.memset(minus1[:, :], -1.0)
            nc.gpsimd.memset(ones[:, :], 1.0)
            nc.gpsimd.memset(eps[:, :], LN_EPS)
            nc.gpsimd.memset(ident[:, :], 0.0).then_inc(s_zero, 1)
            pool.wait_ge(s_zero, 1)
            nc.gpsimd.affine_select(out=ident[:, :], in_=ident[:, :], compare_op=ALU.not_equal, fill=1.0,
                                    base=0, pattern=[[-1, P]], channel_multiplier=1).then_inc(s_ident, 1)
            nc.gpsimd.iota(iota_i[:, :], pattern=[[1, HI]], base=0, channel_multiplier=0).then_inc(s_iota, 1)
            nc.gpsimd.memset(lk_v[:, :, :, :], 1.0)
            nc.gpsimd.memset(xs[:, :, :], 0.0)
            nc.gpsimd.memset(xd[:, :, :], 0.0).then_inc(s_zero, 1)

            def look_up(i, off):
                c, slot = NX * i + off, off % 2
                pool.wait_ge(s_lkix, c + 1)
                pool.sem_inc(s_go)
                for j in range(LK):
                    for k in range(2):
                        nc.gpsimd.indirect_dma_start(
                            lk_v[:, slot, j, k:k + 1], None, table,
                            bass.IndirectOffsetOnAxis(ap=lk_ix[:, slot, j, k:k + 1], axis=0),
                            bounds_check=last_entry, oob_is_err=False).then_inc(s_lk[slot], 16)

            last_entry = pool.to_reg(TABLE - 1)
            last_row = pool.to_reg(N - 1)
            pool.wait_ge(s_zero, 2)
            pool.wait_ge(s_table, 16)
            for c in range(D0):
                look_up(0, c)
            with pool.Fori(0, DPASSES) as i:
                for u in range(NX):
                    look_up(i, D0 + u)
            for c in range(D1, STEPS):
                look_up(0, c)

            def gather(i, off):
                t, slot = ER * i + off, off % ER
                pool.wait_ge(s_gix, t + 1)
                if off >= ER or not isinstance(i, int):
                    pool.wait_ge(s_y, t - ER + 1)
                    pool.wait_ge(s_tt, t - ER + 1)
                pool.sem_inc(s_go)
                for k, buf in enumerate((xs, xd)):
                    nc.gpsimd.indirect_dma_start(
                        buf[:, slot, :], None, x,
                        bass.IndirectOffsetOnAxis(ap=gix[:, slot, k:k + 1], axis=0),
                        bounds_check=last_row, oob_is_err=False).then_inc(s_rowsin[slot], 16)

            def scatter(i, off):
                t, slot = ER * i + off, off % 4
                pool.wait_ge(s_eo, t + 1)
                pool.sem_inc(s_go)
                nc.gpsimd.indirect_dma_start(
                    out, bass.IndirectOffsetOnAxis(ap=six[:, slot, 0:1], axis=0), eo[:, slot, :], None,
                    bounds_check=last_row, oob_is_err=False).then_inc(s_scat[slot], 16)

            for t in range(SCATTER_LAG):
                gather(0, t)
            for slot in range(NX):
                pool.wait_ge(s_store[slot], 16 * (-(-(STEPS - slot) // NX)))
            for t in range(SCATTER_LAG, G0):
                gather(0, t)
                scatter(0, t - SCATTER_LAG)
            with pool.Fori(0, EPASSES) as i:
                for u in range(ER):
                    gather(i, G0 + u)
                    scatter(i, G0 + u - SCATTER_LAG)
            for t in range(G1, TILES + SCATTER_LAG):
                if t < TILES:
                    gather(0, t)
                scatter(0, t - SCATTER_LAG)
            for slot in range(4):
                pool.wait_ge(s_scat[slot], 16 * (TILES // 4))

        @block.scalar
        def _(act):
            act.wait_ge(s_setup, 1)
            nc.scalar.activation(cjunk[:, :], cst[:, 0, :], ACT.Square, accum_out=cn[:, 0:1]).then_inc(s_csq, 1)
            act.wait_ge(s_csq, 1)
            nc.scalar.activation(cn[:, 1:2], cn[:, 0:1], ACT.Sqrt).then_inc(s_csq, 1)
            act.wait_ge(s_clip, 1)
            nc.scalar.activation(root[:, :], root[:, :], ACT.Sqrt).then_inc(s_root, 1)

            def dense_std(i, off):
                c, slot = NX * i + off, off % NX
                pc, rc = parts(c)
                act.wait_ge(s_var, c + 1)
                nc.scalar.activation(std[0:pc, slot, 0:rc], mv[0:pc, slot, 0:rc, 1], ACT.Sqrt,
                                     bias=eps[0:pc, :]).then_inc(s_std, 1)

            def dense_norm(i, off):
                c, slot = NX * i + off, off % NX
                pc, rc = parts(c)
                act.wait_ge(s_rstd, c + 1)
                for r in range(rc):
                    last = nc.scalar.activation(xy[0:pc, slot, r, :], xy[0:pc, slot, r, :], ACT.Identity,
                                                scale=rstd[0:pc, slot, r:r + 1], bias=nmr[0:pc, slot, r:r + 1])
                last.then_inc(s_normed, 1)

            dense_std(0, 0)
            for c in range(1, D0):
                dense_std(0, c)
                dense_norm(0, c - 1)
            with act.Fori(0, DPASSES) as i:
                for u in range(NX):
                    dense_std(i, D0 + u)
                    dense_norm(i, D0 + u - 1)
            for c in range(D1, STEPS):
                dense_std(0, c)
                dense_norm(0, c - 1)
            dense_norm(0, STEPS - 1)

            def take_product(i, off):
                t, slot = ER * i + off, off % 4
                act.wait_ge(s_emb, t + 1)
                if off >= 4 or not isinstance(i, int):
                    act.wait_ge(s_leaky, t - 3)
                nc.scalar.activation(z[:, slot, :], ps_e[off % 2][:, 0:D], ACT.Identity).then_inc(s_z, 1)

            def row_norm(i, off):
                t, slot = ER * i + off, off % 4
                act.wait_ge(s_leaky, t + 1)
                nc.scalar.activation(sq[:, off % 2, :], lr[:, slot, :], ACT.Square,
                                     accum_out=ss[:, slot, 0:1]).then_inc(s_sq, 1)
                act.wait_ge(s_sq, t + 1)
                nc.scalar.activation(ss[:, slot, 1:2], ss[:, slot, 0:1], ACT.Sqrt).then_inc(s_norm, 1)

            def edge_std(i, off):
                t, slot = ER * i + off, off % 4
                act.wait_ge(s_evar, t + 1)
                nc.scalar.activation(esd[:, slot, 0:1], emv[:, slot, 1:2], ACT.Sqrt,
                                     bias=eps[:, :]).then_inc(s_esd, 1)

            def edge_step(i, off, t):
                if t is None or t < TILES:
                    take_product(i, off)
                if t is None or 1 <= t < TILES + 1:
                    row_norm(i, off - 1)
                if t is None or t >= 2:
                    edge_std(i, off - 2)

            for t in range(E0):
                edge_step(0, t, t)
            with act.Fori(0, EPASSES) as i:
                for u in range(ER):
                    edge_step(i, E0 + u, None)
            for t in range(E1, TILES + 2):
                edge_step(0, t, t)

        @block.vector
        def _(dve):
            done = [0]

            def setup(ins):
                done[0] += 1
                ins.then_inc(s_setup, 1)
                dve.wait_ge(s_setup, done[0])

            dve.wait_ge(s_bias, 16)
            setup(nc.vector.scalar_tensor_tensor(out=cst[:, 0, :], in0=bb[:, :], scalar=SLOPE, in1=bb[:, :],
                                                 op0=ALU.mult, op1=ALU.max))
            dve.wait_ge(s_rows, 144)
            nc.vector.tensor_copy(rows_f[:, :, :, :], rows_i[:, :, :, :]).then_inc(s_rows_f, 1)
            dve.wait_ge(s_iota, 1)
            setup(nc.vector.tensor_copy(iota_h[:, :], iota_i[:, :]))
            dve.wait_ge(s_cols, 6)
            setup(nc.vector.tensor_copy(cols[:, 0:2, :].rearrange("p k t -> p (k t)"), ps_t[0][:, 0:2 * TILES]))
            setup(nc.vector.tensor_copy(cols[:, 2, :], ps_t[1][:, 0:TILES]))
            setup(nc.vector.tensor_copy(cols_i[:, :, :], cols[:, 0:2, :]))
            setup(nc.vector.tensor_scalar(hilo_i[:, 0, :, :], cols_i[:, :, :], P - 1, None, ALU.bitwise_and))
            setup(nc.vector.tensor_scalar(hilo_i[:, 1, :, :], cols_i[:, :, :], 7, None, ALU.logical_shift_right))
            setup(nc.vector.tensor_copy(hilo[:, :, :, :], hilo_i[:, :, :, :]))

            def one_hots(i, off):
                t, slot = 2 * i + off, off % 2
                if off >= 2 or not isinstance(i, int):
                    dve.wait_ge(s_hist, t - 1)
                nc.vector.tensor_scalar(oh_lo[:, slot, :], iota_h[:, 0:P], hilo[:, 0, 0, bass.ds(t, 1)], None,
                                        ALU.is_equal)
                nc.vector.tensor_scalar(oh_hi[:, slot, :], iota_h[:, :], hilo[:, 1, 0, bass.ds(t, 1)], None,
                                        ALU.is_equal).then_inc(s_onehot, 1)

            for t in range(2):
                one_hots(0, t)
            with dve.Fori(0, (TILES - 4) // 2) as i:
                for u in range(2):
                    one_hots(i, 2 + u)
            for t in range(TILES - 2, TILES):
                one_hots(0, t)

            for k in range(2):
                setup(nc.vector.scalar_tensor_tensor(out=tix_f[:, :, k], in0=hilo[:, 0, k, :], scalar=float(HI),
                                                     in1=hilo[:, 1, k, :], op0=ALU.mult, op1=ALU.add))
            setup(nc.vector.tensor_copy(tix[:, :, :], tix_f[:, :, :]))
            setup(nc.vector.tensor_tensor(same[:, :], cols[:, 1, :], cols[:, 2, :], ALU.is_equal))
            setup(nc.vector.tensor_copy(rix_f[:, :, 0], cols[:, 0, :]))
            setup(nc.vector.scalar_tensor_tensor(out=rix_f[:, :, 1], in0=same[:, :], scalar=float(SKIP),
                                                 in1=cols[:, 1, :], op0=ALU.mult, op1=ALU.add))
            setup(nc.vector.tensor_copy(rix[:, :, :], rix_f[:, :, :]))
            dve.wait_ge(s_csq, 2)
            setup(nc.vector.tensor_scalar(cn[:, 2:3], cn[:, 1:2], 1e-12, None, ALU.max))
            setup(nc.vector.reciprocal(cn[:, 3:4], cn[:, 2:3]))
            setup(nc.vector.tensor_scalar(cst[:, 0, :], cst[:, 0, :], cn[:, 3:4], None, ALU.mult))
            dve.wait_ge(s_hist, TILES)
            nc.vector.tensor_scalar(root[:, 0:HH], hist[0][:, 0:HH], 1.0, None, ALU.max)
            nc.vector.tensor_scalar(root[:, HH:HI], hist[1][:, 0:HH], 1.0, None, ALU.max).then_inc(s_clip, 1)

            def edge_weight(i, off):
                c, slot = NX * i + off, off % 2
                dve.wait_ge(s_lk[slot], 32 * LK * (lap(NX, 2, i, off) + 1))
                nc.vector.tensor_tensor(lk_p[:, :], lk_v[:, slot, :, 0], lk_v[:, slot, :, 1], ALU.mult).then_inc(s_lkp, 1)
                dve.wait_ge(s_lkp, c + 1)
                nc.vector.reciprocal(weight[:, bass.ds(c * LK, LK)], lk_p[:, :]).then_inc(s_weight, 1)

            def look_up_indices(i, off):
                c, slot = NX * i + off, off % 2
                nc.vector.tensor_copy(lk_ix[:, slot, :, :], tix[:, bass.ds(c * LK, LK), :]).then_inc(s_lkix, 1)

            def dense_stats(i, off):
                c, slot = NX * i + off, off % NX
                pc, rc = parts(c)
                dve.wait_ge(s_load[slot], 16 * (lap(NX, NX, i, off) + 1))
                nc.vector.tensor_tensor(xy[0:pc, slot, 0:rc, :], xy[0:pc, slot, 0:rc, :],
                                        cst[0:pc, :, :].to_broadcast([pc, rc, D]), ALU.add).then_inc(s_added, 1)
                dve.wait_ge(s_added, c + 1)
                for r in range(rc):
                    last = nc.vector.bn_stats(bst[0:pc, off % 2, r, :], xy[0:pc, slot, r, :])
                last.then_inc(s_bst, 1)
                dve.wait_ge(s_bst, c + 1)
                look_up_indices(i, off)
                for r in range(rc):
                    last = nc.vector.bn_aggr(mv[0:pc, slot, r, :], bst[0:pc, off % 2, r, :])
                last.then_inc(s_var, 1)

            def dense_rstd(i, off):
                c, slot = NX * i + off, off % NX
                pc, rc = parts(c)
                dve.wait_ge(s_std, c + 1)
                nc.vector.reciprocal(rstd[0:pc, slot, 0:rc], std[0:pc, slot, 0:rc]).then_inc(s_recip, 1)
                dve.wait_ge(s_recip, c + 1)
                nc.vector.scalar_tensor_tensor(out=nmr[0:pc, slot, 0:rc], in0=mv[0:pc, slot, 0:rc, 0], scalar=-1.0,
                                               in1=rstd[0:pc, slot, 0:rc], op0=ALU.mult, op1=ALU.mult).then_inc(s_rstd, 1)

            for c in range(D0):
                if c >= 2:
                    edge_weight(0, c - 2)
                dense_stats(0, c)
                if c >= 1:
                    dense_rstd(0, c - 1)
            with dve.Fori(0, DPASSES) as i:
                for u in range(NX):
                    edge_weight(i, D0 + u - 2)
                    dense_stats(i, D0 + u)
                    dense_rstd(i, D0 + u - 1)
            for c in range(D1, STEPS + 2):
                edge_weight(0, c - 2)
                if c < STEPS:
                    dense_stats(0, c)
                if c <= STEPS:
                    dense_rstd(0, c - 1)

            def row_indices(i, off):
                t, slot = ER * i + off, off % ER
                nc.vector.tensor_copy(gix[:, slot, :], rix[:, bass.ds(t, 1), :].rearrange("p o k -> p (o k)")).then_inc(s_gix, 1)

            def match_keys(i, off):
                t, slot = ER * i + off, off % 2
                dve.wait_ge(s_kr[off % 4], 16 * (lap(ER, 4, i, off) + 1))
                if off >= 2 or not isinstance(i, int):
                    dve.wait_ge(s_tt, t - 1)
                nc.vector.tensor_scalar(match[:, slot, :], kr[:, off % 4, 1:1 + P], cols[:, 1, bass.ds(t, 1)],
                                        weight[:, bass.ds(t, 1)], ALU.is_equal, ALU.mult)
                nc.vector.tensor_scalar(goes_on[:, slot, :], kr[:, off % 4, 1:1 + P], kr[:, off % 4, 0:1], None,
                                        ALU.is_equal).then_inc(s_match, 1)

            def combine(i, off):
                t, slot = ER * i + off, off % 2
                dve.wait_ge(s_match, t + 1)
                dve.wait_ge(s_tt, t + 1)
                if off >= 1 or not isinstance(i, int):
                    dve.wait_ge(s_tsum, t)
                for k in range(KB):
                    last = nc.vector.scalar_tensor_tensor(
                        out=tsum[:, slot, k, :], in0=goes_on[:, slot, :], scalar=tsum[:, 1 - slot, k, P - 1:P],
                        in1=ps_t[slot][:, k * P:(k + 1) * P], op0=ALU.mult, op1=ALU.add)
                last.then_inc(s_tsum, 1)
                dve.wait_ge(s_tsum, t + 1)
                dve.wait_ge(s_xt, t + 1)
                if off >= 2 or not isinstance(i, int):
                    dve.wait_ge(s_emb, t - 1)
                xt = ps_x[slot][:, 0:D].rearrange("p (k e) -> p k e", k=KB)
                nc.vector.tensor_tensor(ab[:, slot, 0, :, :], tsum[:, slot, :, :], xt, ALU.add)
                nc.vector.tensor_tensor(ab[:, slot, 1, :, :], tsum[:, slot, :, :], xt, ALU.mult).then_inc(s_ab, 1)

            def leaky(i, off):
                t, slot = ER * i + off, off % 4
                dve.wait_ge(s_z, t + 1)
                nc.vector.scalar_tensor_tensor(out=lr[:, slot, :], in0=z[:, slot, :], scalar=SLOPE,
                                               in1=z[:, slot, :], op0=ALU.mult, op1=ALU.max).then_inc(s_leaky, 1)

            def residual(i, off, then_indices):
                t, slot = ER * i + off, off % 4
                dve.wait_ge(s_norm, t + 1)
                nc.vector.tensor_scalar(nr[:, slot, 0:1], ss[:, slot, 1:2], 1e-12, None, ALU.max).then_inc(s_clamp, 1)
                dve.wait_ge(s_clamp, t + 1)
                nc.vector.reciprocal(nr[:, slot, 1:2], nr[:, slot, 0:1]).then_inc(s_unit, 1)
                dve.wait_ge(s_unit, t + 1)
                nc.vector.scalar_tensor_tensor(out=y[:, slot, :], in0=lr[:, slot, :], scalar=nr[:, slot, 1:2],
                                               in1=xd[:, off % ER, :], op0=ALU.mult, op1=ALU.add).then_inc(s_y, 1)
                dve.wait_ge(s_y, t + 1)
                nc.vector.bn_stats(est[:, slot, :], y[:, slot, :]).then_inc(s_est, 1)
                dve.wait_ge(s_est, t + 1)
                if then_indices:
                    row_indices(i, off + 3 + AHEAD)
                nc.vector.bn_aggr(emv[:, slot, :], est[:, slot, :]).then_inc(s_evar, 1)

            def finish(i, off):
                t, slot = ER * i + off, off % 4
                dve.wait_ge(s_esd, t + 1)
                nc.vector.reciprocal(esd[:, slot, 1:2], esd[:, slot, 0:1]).then_inc(s_ers, 1)
                dve.wait_ge(s_ers, t + 1)
                if off >= 4 or not isinstance(i, int):
                    dve.wait_ge(s_scat[slot], 16 * lap(ER, 4, i, off))
                nc.vector.tensor_copy(six[:, slot, :], rix[:, bass.ds(t, 1), 1:2].rearrange("p o k -> p (o k)"))
                nc.vector.tensor_scalar(eo[:, slot, :], y[:, slot, :], emv[:, slot, 0:1], esd[:, slot, 1:2],
                                        ALU.subtract, ALU.mult).then_inc(s_eo, 1)

            nc.vector.memset(tsum[:, 1, :, :], 0.0).then_inc(s_setup, 1)
            dve.wait_ge(s_setup, done[0] + 1)
            dve.wait_ge(s_weight, STEPS)
            for t in range(AHEAD):
                row_indices(0, t)
            match_keys(0, 0)

            def edge_step(i, off, t):
                more = t is None or t + AHEAD < TILES
                if t is not None and t < 3:
                    row_indices(i, off + AHEAD)
                if t is None or t + 1 < TILES:
                    match_keys(i, off + 1)
                if t is None or t < TILES:
                    combine(i, off)
                if t is None or 2 <= t < TILES + 2:
                    leaky(i, off - 2)
                if t is None or 3 <= t < TILES + 3:
                    residual(i, off - 3, more)
                if t is None or t >= 4:
                    finish(i, off - 4)

            for t in range(G0):
                edge_step(0, t, t)
            with dve.Fori(0, EPASSES) as i:
                for u in range(ER):
                    edge_step(i, G0 + u, None)
            for t in range(G1, TILES + 4):
                edge_step(0, t, t)

        @block.tensor
        def _(pe):
            pe.wait_ge(s_rows_f, 1)
            pe.wait_ge(s_ident, 1)
            for k in range(3):
                bank, at = (ps_t[0], k * TILES) if k < 2 else (ps_t[1], 0)
                nc.tensor.transpose(bank[:, at:at + TOP], rows_f[:, k, 0, :], ident[:, :]).then_inc(s_cols, 1)
                nc.tensor.transpose(bank[:, at + TOP:at + TILES], rows_f[0:REST, k, 1, :],
                                    ident[0:REST, 0:REST]).then_inc(s_cols, 1)

            def count_sources(i, off, first=False, last=False):
                t, slot = 2 * i + off, off % 2
                pe.wait_ge(s_onehot, t + 1)
                for k in range(2):
                    ins = nc.tensor.matmul(hist[k][:, 0:HH], oh_lo[:, slot, :], oh_hi[:, slot, k * HH:(k + 1) * HH],
                                           start=first, stop=last)
                ins.then_inc(s_hist, 1)

            for t in range(2):
                count_sources(0, t, first=(t == 0))
            with pe.Fori(0, (TILES - 4) // 2) as i:
                for u in range(2):
                    count_sources(i, 2 + u)
            for t in range(TILES - 2, TILES):
                count_sources(0, t, last=(t == TILES - 1))

            def sum_edges(i, off):
                t, slot = ER * i + off, off % 2
                pe.wait_ge(s_rowsin[off % ER], 32 * (lap(ER, ER, i, off) + 1))
                pe.wait_ge(s_match, t + 1)
                if off >= 2 or not isinstance(i, int):
                    pe.wait_ge(s_tsum, t - 1)
                for k in range(KB):
                    last = nc.tensor.matmul(ps_t[slot][:, k * P:(k + 1) * P], xs[:, off % ER, k * P:(k + 1) * P],
                                            match[:, slot, :], start=True, stop=True)
                last.then_inc(s_tt, 1)
                if off >= 2 or not isinstance(i, int):
                    pe.wait_ge(s_ab, t - 1)
                for k in range(KB):
                    last = nc.tensor.transpose(ps_x[slot][:, k * P:(k + 1) * P], xd[:, off % ER, k * P:(k + 1) * P],
                                               ident[:, :])
                last.then_inc(s_xt, 1)

            def embed(i, off):
                t, slot = ER * i + off, off % 2
                pe.wait_ge(s_ab, t + 1)
                if off >= 2 or not isinstance(i, int):
                    pe.wait_ge(s_z, t - 1)
                for m in range(2):
                    for k in range(KB):
                        nc.tensor.matmul(ps_e[slot][:, 0:D], ab[:, slot, m, k, :], w_sb[:, m, k, :],
                                         start=(m == 0 and k == 0), stop=False)
                nc.tensor.matmul(ps_e[slot][:, 0:D], ones[:, :], brow[:, :], start=False, stop=True).then_inc(s_emb, 1)

            pe.wait_ge(s_w, 48)
            pe.wait_ge(s_zero, 2)
            for t in range(E0):
                sum_edges(0, t)
                if t >= 1:
                    embed(0, t - 1)
            with pe.Fori(0, EPASSES) as i:
                for u in range(ER):
                    sum_edges(i, E0 + u)
                    embed(i, E0 + u - 1)
            for t in range(E1, TILES + 1):
                if t < TILES:
                    sum_edges(0, t)
                embed(0, t - 1)


_INS = ['x', 'src', 'dst', 'L0_gnn_W1', 'L0_gnn_W2', 'L0_gnn_b']
_OUTS = [((100000, 256), 'float32')]


def kernel(**inputs):
    import numpy as _np
    import concourse.bacc as _bacc
    from concourse import mybir as _mybir
    from concourse.bass_utils import run_bass_kernel_spmd as _run

    nc = _bacc.Bacc("TRN2", target_bir_lowering=False, num_devices=1)
    arrays, args = {}, []
    for name in _INS:
        a = _np.ascontiguousarray(inputs[name])
        arrays[f"in_{name}_dram"] = a
        args.append(nc.dram_tensor(f"in_{name}_dram", a.shape, _mybir.dt.from_np(a.dtype), kind="ExternalInput").ap())
    for i, (shape, dtype) in enumerate(_OUTS):
        dt = _mybir.dt.from_np(_np.dtype(dtype))
        args.append(nc.dram_tensor(f"out_{i}_dram", shape, dt, kind="ExternalOutput").ap())
    gnn_resnorm(nc, *args)
    r = _run(nc, [arrays], core_ids=[0])
    got = tuple(r.results[0][f"out_{i}_dram"] for i in range(len(_OUTS)))
    return got[0]
```

```python
def gnn_resnorm(nc, x, src, dst, w1, w2, b, out):
    from contextlib import ExitStack

    import concourse.bass as bass
    from concourse import mybir

    F32, F16, BF16, I32 = mybir.dt.float32, mybir.dt.float16, mybir.dt.bfloat16, mybir.dt.int32
    ALU = mybir.AluOpType
    ACT = mybir.ActivationFunctionType
    P = 128

    N, D = x.shape
    E = src.shape[0]
    KB = D // P
    TE = P - 1
    USED = -(-E // TE)
    PAIRS = -(-USED // 2)
    TILES = 2 * PAIRS
    TOP = P
    REST = TILES - TOP
    E_LAST = E - (USED - 1) * TE
    LO = 2 * P
    HI = -(-N // LO)
    TABLE = LO * HI
    PAD_SRC = TABLE - 1
    PAD_DST = 150000
    SKIP = 1 << 18
    LN_EPS = 1e-5
    SLOPE = 0.01
    assert PAD_SRC >= N and USED == TILES - 1

    R = 8
    NPE = 4
    ROWS = P * R
    CHUNKS = N // ROWS
    LEFT = N - CHUNKS * ROWS
    RL = 7
    PL = LEFT // RL
    STEPS = CHUNKS + 1
    NX = 6
    assert PL * RL == LEFT and PL <= P

    HT = 7
    HSTEPS = USED // HT
    HA, HB = NX, NX + (HSTEPS - NX) // NX * NX
    LK = 3
    GROUPS = TILES // LK
    LS = HSTEPS + 1
    LW = LS + 4
    LA = LW
    LB = LA + (STEPS - 1 - LA) // NX * NX
    SA = 3
    SB = SA + (STEPS - 3 - SA) // NX * NX
    assert HSTEPS * HT == USED - 1 and GROUPS * LK == TILES and GROUPS % NX == 0 and GROUPS + LS <= STEPS

    KP = 22
    K = 2 * KP
    EP = 4
    EA = 8
    EB = EA + (PAIRS - 1 - EA) // EP * EP
    LEAD = KP + 2
    KS = 24
    GP = 3
    DEPTH = 9
    assert KS % 4 == 0 and LEAD + GP * (KP - KS) >= DEPTH and LEAD + GP * KP <= PAIRS

    x_chunks = x[0:CHUNKS * ROWS, :].rearrange("(c p r) d -> c p (r d)", p=P, r=R)
    o_chunks = out[0:CHUNKS * ROWS, :].rearrange("(c p r) d -> c p (r d)", p=P, r=R)
    x_left = x[CHUNKS * ROWS:N, :].rearrange("(p r) d -> p (r d)", r=RL)
    o_left = out[CHUNKS * ROWS:N, :].rearrange("(p r) d -> p (r d)", r=RL)

    table = nc.dram_tensor("degree_root_table", (TABLE, 1), F32).ap()
    keys = nc.dram_tensor("edge_keys", (TILES * P,), F32).ap()

    ctx = ExitStack()
    with ctx:
        def sb(name, shape, dt=F32):
            return ctx.enter_context(nc.sbuf_tensor(name, shape, dt))

        def pb(name, shape, dt=F32):
            return ctx.enter_context(nc.psum_tensor(name, shape, dt))

        def sem(name):
            return ctx.enter_context(nc.semaphore(name))

        def sems(name, n):
            return [sem(f"{name}{k}") for k in range(n)]

        ident = sb("ident", [P, P])
        iota_i = sb("iota_i", [P, HI], I32)
        iota_h = sb("iota_h", [P, HI], F16)
        w_sb = sb("w_sb", [P, 2, KB, D])
        ones3 = sb("ones3", [3, P], BF16)
        eps = sb("eps", [P, 1])
        bb = sb("bb", [P, D])
        cst = sb("cst", [P, 1, D])
        csq = sb("csq", [P, D])
        cn = sb("cn", [P, 4])
        split_f = sb("split_f", [1, 2, 2, D])
        split_h = sb("split_h", [1, 3, 2, D], BF16)
        cb3 = sb("cb3", [3, 2, D], BF16)

        rows_i = sb("rows_i", [P, 3, 2, P], I32)
        rows_f = sb("rows_f", [P, 3, 2, P])
        rows_k = sb("rows_k", [P, 2, P])
        cols = sb("cols", [P, 3, TILES])
        cols_i = sb("cols_i", [P, 2, TILES], I32)
        hilo_i = sb("hilo_i", [P, 2, 2, TILES], I32)
        hilo = sb("hilo", [P, 2, 2, TILES])
        tix_f = sb("tix_f", [P, TILES, 2])
        tix = sb("tix", [P, TILES, 2], I32)
        same = sb("same", [P, TILES])
        rix_f = sb("rix_f", [P, TILES, 2])
        rix = sb("rix", [P, TILES + K, 2], I32)
        weight = sb("weight", [P, TILES])

        oh_lo = sb("oh_lo", [P, HT, LO], F16)
        oh_hi = sb("oh_hi", [P, HT, HI], F16)
        root = sb("root", [P, 2, HI])

        xy = sb("xy", [P, NX, R, D])
        bst = sb("bst", [P, 2, R, 6])
        mv = sb("mv", [P, NX, R, 2])
        std = sb("std", [P, NX, R])
        rstd = sb("rstd", [P, NX, R])
        nmr = sb("nmr", [P, NX, R])
        lk_ix = sb("lk_ix", [P, NX, LK, 2], I32)
        lk_v = sb("lk_v", [P, NX, LK, 2])
        lk_p = sb("lk_p", [P, LK])

        xs = sb("xs", [P, K, D])
        xd = sb("xd", [P, K, D])
        gix = sb("gix", [P, K, 2], I32)
        six = sb("six", [P, 4, 2, 1], I32)
        kr = sb("kr", [P, 4, 2, P])
        match = sb("match", [P, 2, 2, P])
        abt = sb("abt", [P, 2, 2, KB, P])
        sq = sb("sq", [P, D])
        ss = sb("ss", [P, 4, 2])
        nrm = sb("nrm", [P, 4, 2])
        nrc = sb("nrc", [P, 4, 2])
        unit = sb("unit", [P, 4, 2])
        est = sb("est", [P, 2, 2, 6])
        emv = sb("emv", [P, 4, 2, 2])
        esd = sb("esd", [P, 4, 2])
        ers = sb("ers", [P, 4, 2])
        enm = sb("enm", [P, 4, 2])

        FREED = [(STEPS + k) % NX for k in range(3)]
        ab = xy[:, FREED[0], :, :].rearrange("p (s m h) d -> p s m h d", s=2, m=2)
        z = xy[:, FREED[1], 0:4, :].rearrange("p (s h) d -> p s h d", s=2)
        lr = xy[:, FREED[1], 4:8, :].rearrange("p (s h) d -> p s h d", s=2)
        y = xy[:, FREED[2], :, :].rearrange("p (s h) d -> p s h d", s=4)

        ps = [pb(f"ps{k}", [P, 512]) for k in range(8)]
        hist = ps[0:2]
        ps_c = (ps[2:4], ps[4:6], ps[6:8])
        ps_s = ps[0:2]
        ps_x = ps[2:4]
        ps_e = ps[4:6]

        s_zero = sem("s_zero")
        s_ident = sem("s_ident")
        s_iota = sem("s_iota")
        s_go = sem("s_go")
        s_rows = sem("s_rows")
        s_bias = sem("s_bias")
        s_w = sem("s_w")
        s_setup = sem("s_setup")
        s_leakyb = sem("s_leakyb")
        s_rows_f = sem("s_rows_f")
        s_keys = sem("s_keys")
        s_cols = sem("s_cols")
        s_csq = sem("s_csq")
        s_split = sem("s_split")
        s_cb3 = sem("s_cb3")
        s_indices = sem("s_indices")
        s_onehot = sem("s_onehot")
        s_hist = sem("s_hist")
        s_clip = sem("s_clip")
        s_root = sem("s_root")
        s_table = sem("s_table")
        s_load = sems("s_load", NX)
        s_store = sems("s_store", NX)
        s_added = sem("s_added")
        s_added_pe = sem("s_added_pe")
        s_bst = sem("s_bst")
        s_var = sem("s_var")
        s_std = sem("s_std")
        s_recip = sem("s_recip")
        s_rstd = sem("s_rstd")
        s_normed = sem("s_normed")
        s_lkix = sem("s_lkix")
        s_lk = sems("s_lk", NX)
        s_lkp = sem("s_lkp")
        s_weight = sem("s_weight")
        s_gix = sem("s_gix")
        s_rowsin = sems("s_rowsin", 4)
        s_kr = sems("s_kr", 4)
        s_match = sem("s_match")
        s_sum = sem("s_sum")
        s_carry = sem("s_carry")
        s_ab = sem("s_ab")
        s_abt_ps = sem("s_abt_ps")
        s_abt = sem("s_abt")
        s_emb = sem("s_emb")
        s_z = sem("s_z")
        s_leaky = sem("s_leaky")
        s_sq = sem("s_sq")
        s_norm = sem("s_norm")
        s_clamp = sem("s_clamp")
        s_unit = sem("s_unit")
        s_y = sem("s_y")
        s_est = sem("s_est")
        s_evar = sem("s_evar")
        s_esd = sem("s_esd")
        s_ers = sem("s_ers")
        s_enm = sem("s_enm")
        s_done = sem("s_done")
        s_scat = sems("s_scat", 4)

        block = ctx.enter_context(nc.Block())

        def lap(n, k, i, off):
            return (n // k) * i + off // k

        def past(i, off, k):
            return off >= k or not isinstance(i, int)

        def parts(c):
            return (PL, RL) if isinstance(c, int) and c == CHUNKS else (P, R)

        def dense_steps(eng, step, last):
            for c in range(HA):
                step(0, c, c)
            with eng.Fori(0, (HB - HA) // NX) as i:
                for u in range(NX):
                    step(i, HA + u, None)
            for c in range(HB, LA):
                step(0, c, c)
            with eng.Fori(0, (LB - LA) // NX) as i:
                for u in range(NX):
                    step(i, LA + u, None)
            for c in range(LB, last):
                step(0, c, c)

        def pair_steps(eng, step, last):
            for q in range(EA):
                step(0, q, q)
            with eng.Fori(0, (EB - EA) // EP) as i:
                for u in range(EP):
                    step(i, EA + u, None)
            for q in range(EB, last):
                step(0, q, q)

        def dense_slots_left(eng, slots):
            for slot in slots:
                eng.wait_ge(s_store[slot], 16 * (-(-(STEPS - slot) // NX)))

        def runs(q, behind):
            return q is None or 0 <= q - behind < PAIRS

        @block.sync
        def _(sp):
            def load(i, off):
                c, slot = NX * i + off, off % NX
                pc, rc = parts(c)
                if past(i, off, NX):
                    sp.wait_ge(s_store[slot], 16 * lap(NX, NX, i, off))
                sp.dma_start(xy[0:pc, slot, 0:rc, :].rearrange("p r d -> p (r d)"),
                             x_left if pc == PL else x_chunks[c]).then_inc(s_load[slot], 16)

            def store(i, off):
                c, slot = NX * i + off, off % NX
                pc, rc = parts(c)
                sp.wait_ge(s_normed, c + 1)
                sp.dma_start(o_left if pc == PL else o_chunks[c],
                             xy[0:pc, slot, 0:rc, :].rearrange("p r d -> p (r d)")).then_inc(s_store[slot], 16)

            def load_keys(i, off):
                q = EP * i + off
                if past(i, off, 4):
                    sp.wait_ge(s_match, q - 3)
                sp.dma_start(kr[:, off % 4, :, :].rearrange("p t e -> p (t e)"),
                             keys[bass.ds(q * 2 * P, 2 * P)].rearrange("(o e) -> o e", o=1).to_broadcast([P, 2 * P])
                             ).then_inc(s_kr[off % 4], 16)

            sp.dma_start(bb[:, :], b.rearrange("(o d) -> o d", o=1).to_broadcast([P, D])).then_inc(s_bias, 16)
            sp.wait_ge(s_zero, 1)
            for k, (vec, on) in enumerate(((src, 0), (dst, 0), (dst, 1))):
                def shifted_rows(first, tiles, width):
                    return bass.AP(tensor=vec.tensor, offset=first * TE - 1 + on, ap=[[TE, tiles], [1, width]])
                sp.dma_start(rows_i[0:1, k, 0, 1 - on:P],
                             vec[0:P - 1 + on].rearrange("(o e) -> o e", o=1)).then_inc(s_rows, 16)
                sp.dma_start(rows_i[1:P, k, 0, :], shifted_rows(1, TOP - 1, P)).then_inc(s_rows, 16)
                sp.dma_start(rows_i[0:REST - 2, k, 1, :], shifted_rows(TOP, REST - 2, P)).then_inc(s_rows, 16)
                sp.dma_start(rows_i[REST - 2:REST - 1, k, 1, 0:E_LAST + 1 - on],
                             shifted_rows(USED - 1, 1, E_LAST + 1 - on)).then_inc(s_rows, 16)
            for c in range(3):
                load(0, c)
            sp.dma_start(w_sb[:, 0, :, :], w1.rearrange("(k p) n -> p k n", p=P)).then_inc(s_w, 16)
            sp.dma_start(w_sb[:, 1, :, :], w2.rearrange("(k p) n -> p k n", p=P)).then_inc(s_w, 16)
            sp.wait_ge(s_split, 1)
            for k in range(3):
                sp.dma_start(cb3[k:k + 1, :, :].rearrange("p v d -> p (v d)"),
                             split_h[0:1, k, :, :].rearrange("p v d -> p (v d)")).then_inc(s_cb3, 16)

            sp.wait_ge(s_rows_f, 2)
            sp.dma_start(keys[0:TOP * P].rearrange("(t e) -> t e", e=P), rows_k[:, 0, :]).then_inc(s_keys, 16)
            sp.dma_start(keys[TOP * P:TILES * P].rearrange("(t e) -> t e", e=P), rows_k[0:REST, 1, :]).then_inc(s_keys, 16)

            for c in range(SA):
                load(0, c + 3)
                if c >= 1:
                    store(0, c - 1)
            with sp.Fori(0, (SB - SA) // NX) as i:
                for u in range(NX):
                    load(i, SA + u + 3)
                    store(i, SA + u - 1)
            for c in range(SB, STEPS + 1):
                if c + 3 < STEPS:
                    load(0, c + 3)
                store(0, c - 1)

            sp.wait_ge(s_keys, 32)
            for q in range(EP):
                load_keys(0, q)
            with sp.Fori(0, PAIRS // EP - 1) as i:
                for u in range(EP):
                    load_keys(i, EP + u)
            for q in range(PAIRS // EP * EP, PAIRS):
                load_keys(0, q)

        @block.gpsimd
        def _(pool):
            nc.gpsimd.memset(rows_i[:, 0, :, :], PAD_SRC)
            nc.gpsimd.memset(rows_i[:, 1, :, :], PAD_DST)
            nc.gpsimd.memset(rows_i[:, 2, :, :], PAD_DST + 1)
            nc.gpsimd.memset(ones3[:, :], 1.0)
            nc.gpsimd.memset(eps[:, :], LN_EPS)
            nc.gpsimd.memset(ident[:, :], 0.0).then_inc(s_zero, 1)
            pool.wait_ge(s_zero, 1)
            nc.gpsimd.affine_select(out=ident[:, :], in_=ident[:, :], compare_op=ALU.not_equal, fill=1.0,
                                    base=0, pattern=[[-1, P]], channel_multiplier=1).then_inc(s_ident, 1)
            nc.gpsimd.iota(iota_i[:, :], pattern=[[1, HI]], base=0, channel_multiplier=0).then_inc(s_iota, 1)
            nc.gpsimd.memset(rix[:, TILES:TILES + K, :], SKIP)
            nc.gpsimd.memset(lk_v[:, :, :, :], 1.0)
            nc.gpsimd.memset(xs[:, :, :], 0.0)
            nc.gpsimd.memset(xd[:, :, :], 0.0).then_inc(s_zero, 1)

            def gather(i, off):
                p = KP * i + off
                pool.wait_ge(s_gix, p + 1)
                for h in range(2):
                    slot = 2 * (off % KP) + h
                    ring = (2 * off + h) % 4
                    if past(i, off, 2):
                        pool.wait_ge(s_rowsin[ring], 32 * lap(K, 4, i, 2 * off + h))
                    pool.sem_inc(s_go)
                    for k, buf in enumerate((xs, xd)):
                        nc.gpsimd.indirect_dma_start(
                            buf[:, slot, :], None, x,
                            bass.IndirectOffsetOnAxis(ap=gix[:, slot, k:k + 1], axis=0),
                            bounds_check=last_row, oob_is_err=False).then_inc(s_rowsin[ring], 16)

            def look_up(i, off):
                g, slot = NX * i + off, off % NX
                pool.wait_ge(s_lkix, g + 1)
                pool.sem_inc(s_go)
                for j in range(LK):
                    for k in range(2):
                        nc.gpsimd.indirect_dma_start(
                            lk_v[:, slot, j, k:k + 1], None, table,
                            bass.IndirectOffsetOnAxis(ap=lk_ix[:, slot, j, k:k + 1], axis=0),
                            bounds_check=last_entry, oob_is_err=False).then_inc(s_lk[slot], 16)

            def scatter(i, off):
                p, slot = KS * i + off, off % 4
                pool.wait_ge(s_done, p + 1)
                pool.sem_inc(s_go)
                for h in range(2):
                    nc.gpsimd.indirect_dma_start(
                        out, bass.IndirectOffsetOnAxis(ap=six[:, slot, h, 0:1], axis=0), y[:, slot, h, :], None,
                        bounds_check=last_row, oob_is_err=False).then_inc(s_scat[slot], 16)

            last_entry = pool.to_reg(TABLE - 1)
            last_row = pool.to_reg(N - 1)
            pool.wait_ge(s_zero, 2)
            for p in range(KP):
                gather(0, p)
            pool.wait_ge(s_table, 16 * 2)
            with pool.Fori(0, GROUPS // NX) as i:
                for u in range(NX):
                    look_up(i, u)
            for p in range(KP, LEAD):
                gather(0, p)
            dense_slots_left(pool, range(NX))
            with pool.Fori(0, GP) as i:
                gathered = 0
                for u in range(KS):
                    while gathered * KS <= u * KP and gathered < KP:
                        gather(i, LEAD + gathered)
                        gathered += 1
                    scatter(i, u)
            gathered = LEAD + GP * KP
            for u in range(GP * KS, PAIRS):
                if gathered < PAIRS:
                    gather(0, gathered)
                    gathered += 1
                scatter(0, u)
            for slot in range(4):
                pool.wait_ge(s_scat[slot], 32 * (-(-(PAIRS - slot) // 4)))

        @block.scalar
        def _(act):
            act.wait_ge(s_leakyb, 1)
            nc.scalar.activation(csq[:, :], cst[:, 0, :], ACT.Square, accum_out=cn[:, 0:1]).then_inc(s_csq, 1)
            act.wait_ge(s_csq, 1)
            nc.scalar.activation(cn[:, 1:2], cn[:, 0:1], ACT.Sqrt).then_inc(s_csq, 1)

            def dense_std(i, off):
                c, slot = NX * i + off, off % NX
                pc, rc = parts(c)
                act.wait_ge(s_var, c + 1)
                nc.scalar.activation(std[0:pc, slot, 0:rc], mv[0:pc, slot, 0:rc, 1], ACT.Sqrt,
                                     bias=eps[0:pc, :]).then_inc(s_std, 1)

            def dense_norm(i, off):
                c, slot = NX * i + off, off % NX
                pc, rc = parts(c)
                act.wait_ge(s_rstd, c + 1)
                for r in range(rc):
                    xc = ps_c[off % 3][r // 2][0:pc, r % 2 * D:(r % 2 + 1) * D] if r < NPE else xy[0:pc, slot, r, :]
                    last = nc.scalar.activation(xy[0:pc, slot, r, :], xc, ACT.Identity,
                                                scale=rstd[0:pc, slot, r:r + 1], bias=nmr[0:pc, slot, r:r + 1])
                last.then_inc(s_normed, 1)

            def dense_step(i, off, c):
                if c is None or 1 <= c:
                    dense_norm(i, off - 1)
                if c == LS:
                    act.wait_ge(s_clip, 1)
                    nc.scalar.activation(root[:, :, :], root[:, :, :], ACT.Sqrt).then_inc(s_root, 1)
                    act.wait_ge(s_root, 1)
                    for m in range(2):
                        act.dma_start(table[m * P * HI:(m + 1) * P * HI, :].rearrange("(l h) o -> l (h o)", h=HI),
                                      root[:, m, :]).then_inc(s_table, 16)
                if c is None or c < STEPS:
                    dense_std(i, off)

            dense_steps(act, dense_step, STEPS + 1)

            def carry(i, off):
                t, ring = 2 * EP * i + off, off % 2
                act.wait_ge(s_sum, t + 1)
                act.wait_ge(s_rowsin[(off + 1) % 4], 32 * (lap(2 * EP, 4, i, off + 1) + 1))
                nc.scalar.activation(xs[0:1, bass.ds((t + 1) % K, 1), :].rearrange("p o d -> p (o d)"),
                                     ps_s[off // 2 % 2][0:1, ring * D:(ring + 1) * D], ACT.Copy).then_inc(s_carry, 1)

            def operands(i, off):
                t = 2 * EP * i + off
                act.wait_ge(s_abt_ps, t + 1)
                if past(i, off, 2):
                    act.wait_ge(s_emb, t - 1)
                nc.scalar.activation(abt[:, off % 2, :, :, :].rearrange("p m k e -> p (m k e)"), ps_x[off % 2][:, :],
                                     ACT.Copy).then_inc(s_abt, 1)

            def product(i, off):
                q, slot = EP * i + off, off % 2
                act.wait_ge(s_emb, 2 * q + 2)
                if past(i, off, 2):
                    act.wait_ge(s_leaky, q - 1)
                nc.scalar.activation(z[:, slot, :, :].rearrange("p h d -> p (h d)"), ps_e[slot][:, :],
                                     ACT.Copy).then_inc(s_z, 1)

            def norms(i, off):
                q, slot = EP * i + off, off % 4
                act.wait_ge(s_leaky, q + 1)
                for h in range(2):
                    if h == 1:
                        act.wait_ge(s_sq, 2 * q + 1)
                    nc.scalar.activation(sq[:, :], lr[:, off % 2, h, :], ACT.Square,
                                         accum_out=ss[:, slot, h:h + 1]).then_inc(s_sq, 1)
                act.wait_ge(s_sq, 2 * q + 2)
                nc.scalar.activation(nrm[:, slot, :], ss[:, slot, :], ACT.Sqrt).then_inc(s_norm, 1)

            def edge_std(i, off):
                q, slot = EP * i + off, off % 4
                act.wait_ge(s_evar, q + 1)
                nc.scalar.activation(esd[:, slot, :], emv[:, slot, :, 1], ACT.Sqrt, bias=eps[:, :]).then_inc(s_esd, 1)

            def edge_norm(i, off):
                q, slot = EP * i + off, off % 4
                act.wait_ge(s_enm, q + 1)
                for h in range(2):
                    last = nc.scalar.activation(y[:, slot, h, :], y[:, slot, h, :], ACT.Identity,
                                                scale=ers[:, slot, h:h + 1], bias=enm[:, slot, h:h + 1])
                last.then_inc(s_done, 1)

            def pair_step(i, off, q):
                if runs(q, 0):
                    carry(i, 2 * off)
                if runs(q, 2):
                    operands(i, 2 * (off - 2) + 1)
                if runs(q, 3):
                    product(i, off - 3)
                if runs(q, 5):
                    edge_std(i, off - 5)
                if runs(q, 6):
                    edge_norm(i, off - 6)
                if runs(q, 0) and (q is None or q < PAIRS - 1):
                    carry(i, 2 * off + 1)
                if runs(q, 1):
                    operands(i, 2 * (off - 1))
                if runs(q, 3):
                    norms(i, off - 3)

            dense_slots_left(act, FREED[1:2])
            pair_steps(act, pair_step, PAIRS + 6)

        @block.vector
        def _(dve):
            done = [0]

            def setup(ins):
                done[0] += 1
                ins.then_inc(s_setup, 1)
                dve.wait_ge(s_setup, done[0])

            dve.wait_ge(s_bias, 16)
            nc.vector.scalar_tensor_tensor(out=cst[:, 0, :], in0=bb[:, :], scalar=SLOPE, in1=bb[:, :],
                                           op0=ALU.mult, op1=ALU.max).then_inc(s_leakyb, 1)
            dve.wait_ge(s_leakyb, 1)
            dve.wait_ge(s_iota, 1)
            setup(nc.vector.tensor_copy(iota_h[:, :], iota_i[:, :]))
            dve.wait_ge(s_rows, 12 * 16)
            nc.vector.tensor_copy(rows_f[:, :, :, :], rows_i[:, :, :, :]).then_inc(s_rows_f, 1)
            dve.wait_ge(s_rows_f, 1)
            dve.wait_ge(s_csq, 2)
            setup(nc.vector.tensor_scalar(cn[:, 2:3], cn[:, 1:2], 1e-12, None, ALU.max))
            setup(nc.vector.reciprocal(cn[:, 3:4], cn[:, 2:3]))
            setup(nc.vector.tensor_scalar(cst[:, 0, :], cst[:, 0, :], cn[:, 3:4], None, ALU.mult))
            setup(nc.vector.tensor_copy(split_f[:, 0, 0, :], cst[0:1, 0, :]))
            setup(nc.vector.tensor_copy(split_f[:, 0, 1, :], bb[0:1, :]))
            setup(nc.vector.tensor_copy(split_h[:, 0, :, :], split_f[:, 0, :, :]))
            setup(nc.vector.tensor_tensor(split_f[:, 1, :, :], split_f[:, 0, :, :], split_h[:, 0, :, :], ALU.subtract))
            setup(nc.vector.tensor_copy(split_h[:, 1, :, :], split_f[:, 1, :, :]))
            setup(nc.vector.tensor_tensor(split_f[:, 0, :, :], split_f[:, 1, :, :], split_h[:, 1, :, :], ALU.subtract))
            nc.vector.tensor_copy(split_h[:, 2, :, :], split_f[:, 0, :, :]).then_inc(s_split, 1)
            setup(nc.vector.tensor_copy(rows_k[:, :, 1:P], rows_f[:, 1, :, 1:P]))
            nc.vector.tensor_copy(rows_k[:, :, 0:1], rows_f[:, 1, :, P - 1:P]).then_inc(s_rows_f, 1)
            dve.wait_ge(s_cols, 6)
            setup(nc.vector.tensor_copy(cols[:, 0:2, :].rearrange("p k t -> p (k t)"), ps[6][:, 0:2 * TILES]))
            setup(nc.vector.tensor_copy(cols[:, 2, :], ps[7][:, 0:TILES]))
            setup(nc.vector.memset(cols[0:1, 0, :], float(PAD_SRC)))
            setup(nc.vector.tensor_copy(cols_i[:, :, :], cols[:, 0:2, :]))
            setup(nc.vector.tensor_scalar(hilo_i[:, 0, :, :], cols_i[:, :, :], LO - 1, None, ALU.bitwise_and))
            setup(nc.vector.tensor_scalar(hilo_i[:, 1, :, :], cols_i[:, :, :], LO.bit_length() - 1, None, ALU.logical_shift_right))
            setup(nc.vector.tensor_copy(hilo[:, :, :, :], hilo_i[:, :, :, :]))
            setup(nc.vector.tensor_tensor(same[:, :], cols[:, 1, :], cols[:, 2, :], ALU.is_equal))
            setup(nc.vector.memset(same[0:1, :], 1.0))
            setup(nc.vector.tensor_copy(rix_f[:, :, 0], cols[:, 0, :]))
            setup(nc.vector.scalar_tensor_tensor(out=rix_f[:, :, 1], in0=same[:, :], scalar=float(SKIP),
                                                 in1=cols[:, 1, :], op0=ALU.mult, op1=ALU.add))
            setup(nc.vector.tensor_copy(rix[:, 0:TILES, :], rix_f[:, :, :]))
            nc.vector.tensor_copy(gix[:, :, :], rix[:, 0:K, :]).then_inc(s_gix, KP)
            for k in range(2):
                setup(nc.vector.scalar_tensor_tensor(out=tix_f[:, :, k], in0=hilo[:, 0, k, :], scalar=float(HI),
                                                     in1=hilo[:, 1, k, :], op0=ALU.mult, op1=ALU.add))
            setup(nc.vector.tensor_copy(tix[:, :, :], tix_f[:, :, :]))

            def one_hots(i, off, k):
                c = NX * i + off
                t = HT * c + k
                if past(i, off, 1):
                    dve.wait_ge(s_hist, t - HT + 1)
                nc.vector.tensor_scalar(oh_lo[:, k, :], iota_h[:, 0:LO], hilo[:, 0, 0, bass.ds(t, 1)], None,
                                        ALU.is_equal)
                nc.vector.tensor_scalar(oh_hi[:, k, :], iota_h[:, :], hilo[:, 1, 0, bass.ds(t, 1)], None,
                                        ALU.is_equal).then_inc(s_onehot, 1)

            def look_up_indices(i, off):
                g, slot = NX * i + off, off % NX
                nc.vector.tensor_copy(lk_ix[:, slot, :, :], tix[:, bass.ds(g * LK, LK), :]).then_inc(s_lkix, 1)

            def edge_weight(i, off):
                g, slot = NX * i + off, off % NX
                dve.wait_ge(s_lk[slot], 32 * LK * (lap(NX, NX, i, off) + 1))
                nc.vector.tensor_tensor(lk_p[:, :], lk_v[:, slot, :, 0], lk_v[:, slot, :, 1], ALU.mult).then_inc(s_lkp, 1)
                return g

            def edge_weight_end(g):
                dve.wait_ge(s_lkp, g + 1)
                nc.vector.reciprocal(weight[:, bass.ds(g * LK, LK)], lk_p[:, :]).then_inc(s_weight, 1)

            def dense_step(i, off, c):
                n, slot = NX * i + off, off % NX
                pc, rc = parts(n)
                counting = c is None and off < LA or c is not None and c < HSTEPS
                if c is None or c < STEPS:
                    dve.wait_ge(s_load[slot], 16 * (lap(NX, NX, i, off) + 1))
                    nc.vector.tensor_tensor(xy[0:pc, slot, NPE:rc, :], xy[0:pc, slot, NPE:rc, :],
                                            cst[0:pc, :, :].to_broadcast([pc, rc - NPE, D]), ALU.add).then_inc(s_added, 1)
                if counting:
                    for k in range(HT):
                        one_hots(i, off, k)
                if c == HSTEPS:
                    one_hots(0, c, 0)
                if c == LS:
                    dve.wait_ge(s_hist, USED)
                    nc.vector.tensor_scalar(root[:, 0, :], hist[0][:, 0:HI], 1.0, None, ALU.max)
                    nc.vector.tensor_scalar(root[:, 1, :], hist[1][:, 0:HI], 1.0, None, ALU.max).then_inc(s_clip, 1)
                weigh = c is None and off >= LA or c is not None and LW <= c < LW + GROUPS
                if weigh:
                    g = edge_weight(i, off - LW)
                if c is None and off >= LA or c is not None and LS <= c < LS + GROUPS:
                    look_up_indices(i, off - LS)
                if c is None or c < STEPS:
                    dve.wait_ge(s_added_pe, n + 1)
                    for r in range(rc):
                        if r == NPE:
                            dve.wait_ge(s_added, n + 1)
                        xc = ps_c[off % 3][r // 2][0:pc, r % 2 * D:(r % 2 + 1) * D] if r < NPE else xy[0:pc, slot, r, :]
                        last = nc.vector.bn_stats(bst[0:pc, off % 2, r, :], xc)
                    last.then_inc(s_bst, 1)
                if weigh:
                    edge_weight_end(g)
                if c is None or 1 <= c <= STEPS:
                    before = (off - 1) % NX
                    pb_, rb = parts(n - 1)
                    dve.wait_ge(s_std, n)
                    nc.vector.reciprocal(rstd[0:pb_, before, 0:rb], std[0:pb_, before, 0:rb]).then_inc(s_recip, 1)
                if c is None or c < STEPS:
                    dve.wait_ge(s_bst, n + 1)
                if c is None or 1 <= c <= STEPS:
                    dve.wait_ge(s_recip, n)
                    nc.vector.scalar_tensor_tensor(
                        out=nmr[0:pb_, before, 0:rb], in0=mv[0:pb_, before, 0:rb, 0], scalar=-1.0,
                        in1=rstd[0:pb_, before, 0:rb], op0=ALU.mult, op1=ALU.mult).then_inc(s_rstd, 1)
                if c is None or c < STEPS:
                    for r in range(rc):
                        last = nc.vector.bn_aggr(mv[0:pc, slot, r, :], bst[0:pc, off % 2, r, :])
                    last.then_inc(s_var, 1)

            dense_steps(dve, dense_step, max(STEPS, LW + GROUPS - 1) + 1)

            def match_keys(i, off):
                q, slot = EP * i + off, off % 2
                dve.wait_ge(s_kr[off % 4], 16 * (lap(EP, 4, i, off) + 1))
                if past(i, off, 2):
                    dve.wait_ge(s_sum, 2 * q - 2)
                for h in range(2):
                    last = nc.vector.tensor_scalar(
                        match[:, slot, h, :], kr[:, off % 4, h, :], cols[:, 1, bass.ds(2 * q + h, 1)],
                        weight[:, bass.ds(2 * q + h, 1)], ALU.is_equal, ALU.mult)
                last.then_inc(s_match, 1)

            def combine(i, off, carried):
                q, slot = EP * i + off, off % 2
                dve.wait_ge(s_sum, 2 * q + 2)
                dve.wait_ge(s_carry, carried)
                if past(i, off, 2):
                    dve.wait_ge(s_abt_ps, 2 * q - 2)
                sums = ps_s[slot][:, :].rearrange("p (h d) -> p h d", h=2)
                xds = xd[:, bass.ds((2 * q) % K, 2), :]
                nc.vector.tensor_tensor(ab[:, slot, 0, :, :], sums, xds, ALU.add)
                nc.vector.tensor_tensor(ab[:, slot, 1, :, :], sums, xds, ALU.mult).then_inc(s_ab, 1)

            def leaky(i, off):
                q, slot = EP * i + off, off % 2
                dve.wait_ge(s_z, q + 1)
                nc.vector.scalar_tensor_tensor(
                    out=lr[:, slot, :, :].rearrange("p h d -> p (h d)"), in0=z[:, slot, :, :].rearrange("p h d -> p (h d)"),
                    scalar=SLOPE, in1=z[:, slot, :, :].rearrange("p h d -> p (h d)"), op0=ALU.mult,
                    op1=ALU.max).then_inc(s_leaky, 1)

            def pair_step(i, off, q):
                n = EP * i + off
                slot4, slot6 = (off - 4) % 4, (off - 6) % 4
                m = n - 4
                if runs(q, 4):
                    dve.wait_ge(s_norm, m + 1)
                    nc.vector.tensor_scalar(nrc[:, slot4, :], nrm[:, slot4, :], 1e-12, None, ALU.max).then_inc(s_clamp, 1)
                if runs(q, 6):
                    dve.wait_ge(s_esd, n - 5)
                    nc.vector.reciprocal(ers[:, slot6, :], esd[:, slot6, :]).then_inc(s_ers, 1)
                if runs(q, 4):
                    dve.wait_ge(s_clamp, m + 1)
                    nc.vector.reciprocal(unit[:, slot4, :], nrc[:, slot4, :]).then_inc(s_unit, 1)
                if runs(q, 6):
                    dve.wait_ge(s_ers, n - 5)
                    nc.vector.scalar_tensor_tensor(
                        out=enm[:, slot6, :], in0=emv[:, slot6, :, 0], scalar=-1.0, in1=ers[:, slot6, :],
                        op0=ALU.mult, op1=ALU.mult).then_inc(s_enm, 1)
                if runs(q, -1):
                    match_keys(i, off + 1)
                if runs(q, 4):
                    if past(i, off, 8):
                        dve.wait_ge(s_scat[slot4], 32 * lap(EP, 4, i, off - 4))
                    nc.vector.tensor_copy(six[:, slot4, :, :], rix[:, bass.ds(2 * m, 2), 1:2])
                    dve.wait_ge(s_unit, m + 1)
                    for h in range(2):
                        last = nc.vector.scalar_tensor_tensor(
                            out=y[:, slot4, h, :], in0=lr[:, off % 2, h, :], scalar=unit[:, slot4, h:h + 1],
                            in1=xd[:, bass.ds((2 * m + h) % K, 1), :].rearrange("p o d -> p (o d)"),
                            op0=ALU.mult, op1=ALU.add)
                    last.then_inc(s_y, 1)
                if runs(q, 3):
                    leaky(i, off - 3)
                if runs(q, 4):
                    dve.wait_ge(s_y, m + 1)
                    for h in range(2):
                        last = nc.vector.bn_stats(est[:, off % 2, h, :], y[:, slot4, h, :])
                    last.then_inc(s_est, 1)
                if runs(q, 0):
                    combine(i, off, 2 * PAIRS - 1 if q == PAIRS - 1 else 2 * n + 2)
                if runs(q, 4):
                    dve.wait_ge(s_est, m + 1)
                    if q is None or m + KP < PAIRS:
                        nc.vector.tensor_copy(gix[:, bass.ds((2 * m) % K, 2), :],
                                              rix[:, bass.ds(2 * m + K, 2), :]).then_inc(s_gix, 1)
                    for h in range(2):
                        last = nc.vector.bn_aggr(emv[:, slot4, h, :], est[:, off % 2, h, :])
                    last.then_inc(s_evar, 1)

            dve.wait_ge(s_weight, GROUPS)
            dense_slots_left(dve, FREED)
            setup(nc.vector.memset(weight[0:1, :], 1.0))
            match_keys(0, 0)
            pair_steps(dve, pair_step, PAIRS + 6)

        @block.tensor
        def _(pe):
            pe.wait_ge(s_rows_f, 1)
            pe.wait_ge(s_ident, 1)
            for k in range(3):
                bank, at = (ps[6], k * TILES) if k < 2 else (ps[7], 0)
                nc.tensor.transpose(bank[:, at:at + TOP], rows_f[:, k, 0, :], ident[:, :]).then_inc(s_cols, 1)
                nc.tensor.transpose(bank[:, at + TOP:at + TILES], rows_f[0:REST, k, 1, :],
                                    ident[0:REST, 0:REST]).then_inc(s_cols, 1)

            def count_sources(i, off, k, first=False, last=False):
                t = HT * (NX * i + off) + k
                pe.wait_ge(s_onehot, t + 1)
                for m in range(2):
                    ins = nc.tensor.matmul(hist[m][:, 0:HI], oh_lo[:, k, m * P:(m + 1) * P], oh_hi[:, k, :],
                                           start=first, stop=last)
                ins.then_inc(s_hist, 1)

            def dense_step(i, off, c):
                n, slot = NX * i + off, off % NX
                pc, rc = parts(n)
                if c == 0:
                    pe.wait_ge(s_cb3, 48)
                if c is None or c < STEPS:
                    pe.wait_ge(s_load[slot], 16 * (lap(NX, NX, i, off) + 1))
                    if past(i, off, 3):
                        pe.wait_ge(s_normed, n - 2)
                    for r in range(NPE):
                        acc = ps_c[off % 3][r // 2][0:pc, r % 2 * D:(r % 2 + 1) * D]
                        nc.tensor.matmul(acc, ident[0:pc, 0:pc], xy[0:pc, slot, r, :], start=True, stop=False)
                        last = nc.tensor.matmul(acc, ones3[:, 0:pc], cb3[:, 0, :], start=False, stop=True)
                    last.then_inc(s_added_pe, 1)
                if c is None and off < LA or c is not None and c < HSTEPS:
                    for k in range(HT):
                        count_sources(i, off, k, first=(c == 0 and k == 0))
                if c == HSTEPS:
                    count_sources(0, c, 0, last=True)

            dense_steps(pe, dense_step, STEPS)

            def sum_edges(i, off):
                t, slot, half = 2 * EP * i + off, off // 2 % 2, off % 2
                if half == 0:
                    pe.wait_ge(s_match, EP * i + off // 2 + 1)
                    if past(i, off, 4):
                        pe.wait_ge(s_ab, EP * i + off // 2 - 1)
                pe.wait_ge(s_rowsin[off % 4], 32 * (lap(2 * EP, 4, i, off) + 1))
                if past(i, off, 1):
                    pe.wait_ge(s_carry, t)
                nc.tensor.matmul(ps_s[slot][:, half * D:(half + 1) * D], match[:, slot, half, :],
                                 xs[:, bass.ds(t % K, 1), :].rearrange("p o d -> p (o d)"), start=True,
                                 stop=True).then_inc(s_sum, 1)

            def transposes(i, off):
                t, slot, half = 2 * EP * i + off, off // 2 % 2, off % 2
                if half == 0:
                    pe.wait_ge(s_ab, EP * i + off // 2 + 1)
                if past(i, off, 2):
                    pe.wait_ge(s_abt, t - 1)
                for m in range(2):
                    for k in range(KB):
                        at = (m * KB + k) * P
                        last = nc.tensor.transpose(ps_x[half][:, at:at + P], ab[:, slot, m, half, k * P:(k + 1) * P],
                                                   ident[:, :])
                last.then_inc(s_abt_ps, 1)

            def products(i, off):
                t, slot, half = 2 * EP * i + off, off // 2 % 2, off % 2
                pe.wait_ge(s_abt, t + 1)
                if half == 0 and past(i, off, 4):
                    pe.wait_ge(s_z, EP * i + off // 2 - 1)
                acc = ps_e[slot][:, half * D:(half + 1) * D]
                for m in range(2):
                    for k in range(KB):
                        nc.tensor.matmul(acc, abt[:, half, m, k, :], w_sb[:, m, k, :],
                                         start=(m == 0 and k == 0), stop=False)
                nc.tensor.matmul(acc, ones3[:, :], cb3[:, 1, :], start=False, stop=True).then_inc(s_emb, 1)

            def pair_step(i, off, q):
                if runs(q, 0):
                    sum_edges(i, 2 * off)
                if runs(q, 2):
                    transposes(i, 2 * (off - 2) + 1)
                    products(i, 2 * (off - 2))
                if runs(q, 0):
                    sum_edges(i, 2 * off + 1)
                if runs(q, 1):
                    transposes(i, 2 * (off - 1))
                if runs(q, 2):
                    products(i, 2 * (off - 2) + 1)

            pe.wait_ge(s_w, 32)
            pe.wait_ge(s_zero, 2)
            pe.wait_ge(s_clip, 1)
            pe.wait_ge(s_normed, STEPS)
            pair_steps(pe, pair_step, PAIRS + 2)


_INS = ['x', 'src', 'dst', 'L0_gnn_W1', 'L0_gnn_W2', 'L0_gnn_b']
_OUTS = [((100000, 256), 'float32')]


def kernel(**inputs):
    import numpy as _np
    import concourse.bacc as _bacc
    from concourse import mybir as _mybir
    from concourse.bass_utils import run_bass_kernel_spmd as _run

    nc = _bacc.Bacc("TRN2", target_bir_lowering=False, num_devices=1)
    arrays, args = {}, []
    for name in _INS:
        a = _np.ascontiguousarray(inputs[name])
        arrays[f"in_{name}_dram"] = a
        args.append(nc.dram_tensor(f"in_{name}_dram", a.shape, _mybir.dt.from_np(a.dtype), kind="ExternalInput").ap())
    for i, (shape, dtype) in enumerate(_OUTS):
        dt = _mybir.dt.from_np(_np.dtype(dtype))
        args.append(nc.dram_tensor(f"out_{i}_dram", shape, dt, kind="ExternalOutput").ap())
    gnn_resnorm(nc, *args)
    r = _run(nc, [arrays], core_ids=[0])
    got = tuple(r.results[0][f"out_{i}_dram"] for i in range(len(_OUTS)))
    return got[0]
```

```python
def gnn_resnorm(nc, x, src, dst, w1, w2, b, out):
    from contextlib import ExitStack

    import concourse.bass as bass
    from concourse import mybir

    F32, F16, BF16, I32 = mybir.dt.float32, mybir.dt.float16, mybir.dt.bfloat16, mybir.dt.int32
    ALU = mybir.AluOpType
    ACT = mybir.ActivationFunctionType
    P = 128

    N, D = x.shape
    E = src.shape[0]
    KB = D // P
    TE = P - 1
    USED = -(-E // TE)
    PAIRS = -(-USED // 2)
    TILES = 2 * PAIRS
    TOP = P
    REST = TILES - TOP
    E_LAST = E - (USED - 1) * TE
    LO = 2 * P
    HI = -(-N // LO)
    TABLE = LO * HI
    PAD_SRC = TABLE - 1
    PAD_DST = N + N // 2
    SKIP = 1 << 18
    LN_EPS = 1e-5
    SLOPE = 0.01
    assert PAD_SRC >= N and USED == TILES - 1

    R = 8
    NPE_COUNT, NPE, NPE_TAIL = 6, 4, 2
    ROWS = P * R
    CHUNKS = N // ROWS
    LEFT = N - CHUNKS * ROWS
    RL = 7
    PL = LEFT // RL
    STEPS = CHUNKS + 1
    NX = 6
    assert PL * RL == LEFT and PL <= P

    HT = 7
    HSTEPS = USED // HT
    HA, HB = NX, NX + (HSTEPS - NX) // NX * NX
    LK = 3
    GROUPS = TILES // LK
    LS = HSTEPS + 1
    LW = LS + 4
    LA = LW
    LB = LA + (STEPS - 1 - LA) // NX * NX - NX
    TAIL = LB
    TAIL_PAIRS = {TAIL + 1: 0, TAIL + 3: 1, TAIL + 5: 2, TAIL + 7: 3, TAIL + 9: 4, TAIL + 10: 5, TAIL + 11: 6}
    SA = 3
    SB = SA + (TAIL - SA) // NX * NX
    assert HSTEPS * HT == USED - 1 and GROUPS * LK == TILES and GROUPS % NX == 0 and GROUPS + LS <= STEPS
    assert LW + GROUPS - 1 <= STEPS

    KP = 28
    K = 2 * KP
    EP = 4
    EA = 8
    EB = EA + (PAIRS - 1 - EA) // EP * EP
    LEAD = KP + 2
    KS = 36
    GP = 2
    DEPTH = 9
    assert KS % 4 == 0 and LEAD + GP * (KP - KS) >= DEPTH and LEAD + GP * KP <= PAIRS

    x_chunks = x[0:CHUNKS * ROWS, :].rearrange("(c p r) d -> c p (r d)", p=P, r=R)
    o_chunks = out[0:CHUNKS * ROWS, :].rearrange("(c p r) d -> c p (r d)", p=P, r=R)
    x_left = x[CHUNKS * ROWS:N, :].rearrange("(p r) d -> p (r d)", r=RL)
    o_left = out[CHUNKS * ROWS:N, :].rearrange("(p r) d -> p (r d)", r=RL)

    table = nc.dram_tensor("degree_root_table", (TABLE, 1), F32).ap()
    keys = nc.dram_tensor("edge_keys", (TILES * P,), F32).ap()

    ctx = ExitStack()
    with ctx:
        def sb(name, shape, dt=F32, stack=ctx):
            return stack.enter_context(nc.sbuf_tensor(name, shape, dt))

        def pb(name, shape, dt=F32):
            return ctx.enter_context(nc.psum_tensor(name, shape, dt))

        def sem(name):
            return ctx.enter_context(nc.semaphore(name))

        def sems(name, n):
            return [sem(f"{name}{k}") for k in range(n)]

        ident = sb("ident", [P, P])
        w_sb = sb("w_sb", [P, 2, KB, D])
        ones3 = sb("ones3", [3, P], BF16)
        eps = sb("eps", [P, 1])
        bb = sb("bb", [P, 1, D])
        cst = sb("cst", [P, 1, D])
        cb3 = sb("cb3", [3, D], BF16)

        cols = sb("cols", [P, 3, TILES])
        tix = sb("tix", [P, TILES, 2], I32)
        rix = sb("rix", [P, TILES + K, 2], I32)
        weight = sb("weight", [P, TILES])


        xy = sb("xy", [P, NX, R, D])
        bst = sb("bst", [P, 2, R, 6])
        mv = sb("mv", [P, NX, R, 2])
        std = sb("std", [P, NX, R])
        rstd = sb("rstd", [P, NX, R])
        nmr = sb("nmr", [P, NX, R])
        lk_ix = sb("lk_ix", [P, NX, LK, 2], I32)
        lk_v = sb("lk_v", [P, NX, LK, 2])
        lk_p = sb("lk_p", [P, LK])

        xs = sb("xs", [P, K, D])
        xd = sb("xd", [P, K, D])
        gix = sb("gix", [P, K, 2], I32)
        six = sb("six", [P, 4, 2, 1], I32)
        kr = sb("kr", [P, 4, 2, P])
        ss = sb("ss", [P, 4, 2])
        nrm = sb("nrm", [P, 4, 2])
        nrc = sb("nrc", [P, 4, 2])
        unit = sb("unit", [P, 4, 2])
        est = sb("est", [P, 2, 2, 6])
        emv = sb("emv", [P, 4, 2, 2])
        esd = sb("esd", [P, 4, 2])
        ers = sb("ers", [P, 4, 2])
        enm = sb("enm", [P, 4, 2])

        with ExitStack() as early:
            iota_h = sb("iota_h", [P, HI], F16, stack=early)
            hilo = sb("hilo", [P, 2, 2, TILES], stack=early)
            with ExitStack() as shared:
                iota_i = sb("iota_i", [P, HI], I32, stack=shared)
                csq = sb("csq", [P, D], stack=shared)
                cn = sb("cn", [P, 4], stack=shared)
                split_f = sb("split_f", [1, 2, D], stack=shared)
                split_h = sb("split_h", [1, 3, D], BF16, stack=shared)
                rows_i = sb("rows_i", [P, 3, 2, P], I32, stack=shared)
                rows_f = sb("rows_f", [P, 3, 2, P], stack=shared)
                rows_k = sb("rows_k", [P, 2, P], stack=shared)
                cols_i = sb("cols_i", [P, 2, TILES], I32, stack=shared)
                hilo_i = sb("hilo_i", [P, 2, 2, TILES], I32, stack=shared)
                same = sb("same", [P, TILES], stack=shared)
            with ExitStack() as shared:
                oh_lo = sb("oh_lo", [P, HT, LO], F16, stack=shared)
                oh_hi = sb("oh_hi", [P, HT, HI], F16, stack=shared)
                root = sb("root", [P, 2, HI], stack=shared)
        match = sb("match", [P, 2, 2, P])
        ab = sb("ab", [P, 2, 2, 2, D])
        abt = sb("abt", [P, 2, 2, KB, P])
        z = sb("z", [P, 2, 2, D])
        sq = sb("sq", [P, D])
        y = sb("y", [P, 4, 2, D])

        ps = [pb(f"ps{k}", [P, 512]) for k in range(8)]
        hist = ps[0:2]
        ps_count = (ps[2:5], ps[5:8])
        ps_c = (ps[2:4], ps[4:6], ps[6:8])
        ps_s = ps[0:2]
        ps_tail, ps_x, ps_e = (ps_c[(TAIL - k - HSTEPS) % 3] for k in (2, 1, 3))

        s_zero = sem("s_zero")
        s_ident = sem("s_ident")
        s_iota = sem("s_iota")
        s_go = sem("s_go")
        s_rows = sem("s_rows")
        s_bias = sem("s_bias")
        s_w = sem("s_w")
        s_setup = sem("s_setup")
        s_leakyb = sem("s_leakyb")
        s_rows_f = sem("s_rows_f")
        s_keys = sem("s_keys")
        s_cols = sem("s_cols")
        s_csq = sem("s_csq")
        s_split = sem("s_split")
        s_cb3 = sem("s_cb3")
        s_onehot = sem("s_onehot")
        s_hist = sem("s_hist")
        s_clip = sem("s_clip")
        s_root = sem("s_root")
        s_table = sem("s_table")
        s_load = sems("s_load", NX)
        s_store = sems("s_store", NX)
        s_added = sem("s_added")
        s_added_pe = sem("s_added_pe")
        s_bst = sem("s_bst")
        s_var = sem("s_var")
        s_std = sem("s_std")
        s_recip = sem("s_recip")
        s_rstd = sem("s_rstd")
        s_normed = sem("s_normed")
        s_lkix = sem("s_lkix")
        s_lk = sems("s_lk", NX)
        s_lkp = sem("s_lkp")
        s_weight = sem("s_weight")
        s_gix = sem("s_gix")
        s_rowsin = sems("s_rowsin", 4)
        s_kr = sems("s_kr", 4)
        s_match = sem("s_match")
        s_sum = sem("s_sum")
        s_carry = sem("s_carry")
        s_ab = sem("s_ab")
        s_abt_ps = sem("s_abt_ps")
        s_abt = sem("s_abt")
        s_emb = sem("s_emb")
        s_z = sem("s_z")
        s_leaky = sem("s_leaky")
        s_sq = sem("s_sq")
        s_norm = sem("s_norm")
        s_clamp = sem("s_clamp")
        s_unit = sem("s_unit")
        s_y = sem("s_y")
        s_est = sem("s_est")
        s_evar = sem("s_evar")
        s_esd = sem("s_esd")
        s_ers = sem("s_ers")
        s_enm = sem("s_enm")
        s_done = sem("s_done")
        s_scat = sems("s_scat", 4)

        block = ctx.enter_context(nc.Block())

        def lap(n, k, i, off):
            return (n // k) * i + off // k

        def past(i, off, k):
            return off >= k or not isinstance(i, int)

        def by_pe(off):
            return NPE_COUNT if off < HSTEPS else NPE if off < TAIL else NPE_TAIL

        assert HSTEPS % 2 == 0

        def added(off, r, pc):
            if off < HSTEPS:
                banks = ps_count[off % 2]
            elif off < TAIL:
                banks = ps_c[(off - HSTEPS) % 3]
            else:
                banks = (ps_tail[(off - TAIL) % 2],)
            return banks[r // 2][0:pc, r % 2 * D:(r % 2 + 1) * D]

        def parts(c):
            return (PL, RL) if isinstance(c, int) and c == CHUNKS else (P, R)

        def dense_steps(eng, step):
            for c in range(HA):
                step(0, c, c)
            with eng.Fori(0, (HB - HA) // NX) as i:
                for u in range(NX):
                    step(i, HA + u, None)
            for c in range(HB, LA):
                step(0, c, c)
            with eng.Fori(0, (LB - LA) // NX) as i:
                for u in range(NX):
                    step(i, LA + u, None)

        def tail_steps(dense_step, pair_step, last):
            for c in range(TAIL, STEPS + 1):
                if c <= last:
                    dense_step(0, c, c)
                if c in TAIL_PAIRS:
                    pair_step(0, TAIL_PAIRS[c], TAIL_PAIRS[c])

        def pair_steps(eng, step, last):
            for q in range(len(TAIL_PAIRS), EA):
                step(0, q, q)
            with eng.Fori(0, (EB - EA) // EP) as i:
                for u in range(EP):
                    step(i, EA + u, None)
            for q in range(EB, last):
                step(0, q, q)

        def runs(q, behind):
            return q is None or 0 <= q - behind < PAIRS

        @block.sync
        def _(sp):
            def load(i, off):
                c, slot = NX * i + off, off % NX
                pc, rc = parts(c)
                if past(i, off, NX):
                    sp.wait_ge(s_store[slot], 16 * lap(NX, NX, i, off))
                sp.dma_start(xy[0:pc, slot, 0:rc, :].rearrange("p r d -> p (r d)"),
                             x_left if pc == PL else x_chunks[c]).then_inc(s_load[slot], 16)

            def store(i, off):
                c, slot = NX * i + off, off % NX
                pc, rc = parts(c)
                sp.wait_ge(s_normed, c + 1)
                sp.dma_start(o_left if pc == PL else o_chunks[c],
                             xy[0:pc, slot, 0:rc, :].rearrange("p r d -> p (r d)")).then_inc(s_store[slot], 16)

            def load_keys(i, off):
                q = EP * i + off
                if past(i, off, 4):
                    sp.wait_ge(s_match, q - 3)
                sp.dma_start(kr[:, off % 4, :, :].rearrange("p t e -> p (t e)"),
                             keys[bass.ds(q * 2 * P, 2 * P)].rearrange("(o e) -> o e", o=1).to_broadcast([P, 2 * P])
                             ).then_inc(s_kr[off % 4], 16)

            sp.dma_start(bb[:, 0, :], b.rearrange("(o d) -> o d", o=1).to_broadcast([P, D])).then_inc(s_bias, 16)
            sp.wait_ge(s_zero, 1)
            for k, (vec, on) in enumerate(((src, 0), (dst, 0), (dst, 1))):
                def shifted_rows(first, tiles, width):
                    return bass.AP(tensor=vec.tensor, offset=first * TE - 1 + on, ap=[[TE, tiles], [1, width]])
                sp.dma_start(rows_i[0:1, k, 0, 1 - on:P],
                             vec[0:P - 1 + on].rearrange("(o e) -> o e", o=1)).then_inc(s_rows, 16)
                sp.dma_start(rows_i[1:P, k, 0, :], shifted_rows(1, TOP - 1, P)).then_inc(s_rows, 16)
                sp.dma_start(rows_i[0:REST - 2, k, 1, :], shifted_rows(TOP, REST - 2, P)).then_inc(s_rows, 16)
                sp.dma_start(rows_i[REST - 2:REST - 1, k, 1, 0:E_LAST + 1 - on],
                             shifted_rows(USED - 1, 1, E_LAST + 1 - on)).then_inc(s_rows, 16)
            for c in range(3):
                load(0, c)
            sp.wait_ge(s_split, 1)
            for k in range(3):
                sp.dma_start(cb3[k:k + 1, :], split_h[0:1, k, :]).then_inc(s_cb3, 16)

            sp.wait_ge(s_rows_f, 2)
            sp.dma_start(keys[0:TOP * P].rearrange("(t e) -> t e", e=P), rows_k[:, 0, :]).then_inc(s_keys, 16)
            sp.dma_start(keys[TOP * P:TILES * P].rearrange("(t e) -> t e", e=P), rows_k[0:REST, 1, :]).then_inc(s_keys, 16)

            for c in range(3, SA + 3):
                load(0, c)
            for c in range(1, SA):
                store(0, c - 1)
            sp.dma_start(w_sb[:, 0, :, :], w1.rearrange("(k p) n -> p k n", p=P)).then_inc(s_w, 16)
            sp.dma_start(w_sb[:, 1, :, :], w2.rearrange("(k p) n -> p k n", p=P)).then_inc(s_w, 16)
            sp.wait_ge(s_keys, 32)
            for q in range(EP):
                load_keys(0, q)
            with sp.Fori(0, (SB - SA) // NX) as i:
                for u in range(NX):
                    load(i, SA + u + 3)
                    store(i, SA + u - 1)
            for c in range(SB, STEPS + 1):
                if c + 3 < STEPS:
                    load(0, c + 3)
                store(0, c - 1)
                if c in TAIL_PAIRS:
                    load_keys(0, TAIL_PAIRS[c] + EP)

            for q in range(len(TAIL_PAIRS) + EP, EA + EP):
                load_keys(0, q)
            with sp.Fori(0, (PAIRS - EA) // EP - 1) as i:
                for u in range(EP):
                    load_keys(i, EA + EP + u)
            for q in range(PAIRS // EP * EP, PAIRS):
                load_keys(0, q)

        @block.gpsimd
        def _(pool):
            nc.gpsimd.memset(rows_i[:, 0, :, :], PAD_SRC)
            nc.gpsimd.memset(rows_i[:, 1, :, :], PAD_DST)
            nc.gpsimd.memset(rows_i[:, 2, :, :], PAD_DST + 1)
            nc.gpsimd.memset(ones3[:, :], 1.0)
            nc.gpsimd.memset(eps[:, :], LN_EPS)
            nc.gpsimd.memset(ident[:, :], 0.0).then_inc(s_zero, 1)
            pool.wait_ge(s_zero, 1)
            nc.gpsimd.affine_select(out=ident[:, :], in_=ident[:, :], compare_op=ALU.not_equal, fill=1.0,
                                    base=0, pattern=[[-1, P]], channel_multiplier=1).then_inc(s_ident, 1)
            nc.gpsimd.iota(iota_i[:, :], pattern=[[1, HI]], base=0, channel_multiplier=0).then_inc(s_iota, 1)
            nc.gpsimd.memset(rix[:, TILES:TILES + K, :], SKIP)
            nc.gpsimd.memset(lk_v[:, :, :, :], 1.0)
            nc.gpsimd.memset(xs[:, :, :], 0.0)
            nc.gpsimd.memset(xd[:, :, :], 0.0).then_inc(s_zero, 1)

            def gather(i, off):
                p = KP * i + off
                pool.wait_ge(s_gix, p + 1)
                for h in range(2):
                    slot = 2 * (off % KP) + h
                    ring = (2 * off + h) % 4
                    if past(i, off, 2):
                        pool.wait_ge(s_rowsin[ring], 32 * lap(K, 4, i, 2 * off + h))
                    pool.sem_inc(s_go)
                    for k, buf in enumerate((xs, xd)):
                        nc.gpsimd.indirect_dma_start(
                            buf[:, slot, :], None, x,
                            bass.IndirectOffsetOnAxis(ap=gix[:, slot, k:k + 1], axis=0),
                            bounds_check=last_row, oob_is_err=False).then_inc(s_rowsin[ring], 16)

            def look_up(i, off):
                g, slot = NX * i + off, off % NX
                pool.wait_ge(s_lkix, g + 1)
                pool.sem_inc(s_go)
                for j in range(LK):
                    for k in range(2):
                        nc.gpsimd.indirect_dma_start(
                            lk_v[:, slot, j, k:k + 1], None, table,
                            bass.IndirectOffsetOnAxis(ap=lk_ix[:, slot, j, k:k + 1], axis=0),
                            bounds_check=last_entry, oob_is_err=False).then_inc(s_lk[slot], 16)

            def scatter(i, off):
                p, slot = KS * i + off, off % 4
                pool.wait_ge(s_done, p + 1)
                pool.sem_inc(s_go)
                for h in range(2):
                    nc.gpsimd.indirect_dma_start(
                        out, bass.IndirectOffsetOnAxis(ap=six[:, slot, h, 0:1], axis=0), y[:, slot, h, :], None,
                        bounds_check=last_row, oob_is_err=False).then_inc(s_scat[slot], 16)

            last_entry = pool.to_reg(TABLE - 1)
            last_row = pool.to_reg(N - 1)
            pool.wait_ge(s_zero, 2)
            for p in range(KP):
                gather(0, p)
            pool.wait_ge(s_table, 16 * 2)
            with pool.Fori(0, GROUPS // NX) as i:
                for u in range(NX):
                    look_up(i, u)
            for p in range(KP, LEAD):
                gather(0, p)
            for slot in range(NX):
                pool.wait_ge(s_store[slot], 16 * (-(-(STEPS - slot) // NX)))
            with pool.Fori(0, GP) as i:
                gathered = 0
                for u in range(KS):
                    while gathered * KS <= u * KP and gathered < KP:
                        gather(i, LEAD + gathered)
                        gathered += 1
                    scatter(i, u)
            gathered = LEAD + GP * KP
            for u in range(GP * KS, PAIRS):
                if gathered < PAIRS and u % 4 != 3:
                    gather(0, gathered)
                    gathered += 1
                scatter(0, u)
            for slot in range(4):
                pool.wait_ge(s_scat[slot], 32 * (-(-(PAIRS - slot) // 4)))

        @block.scalar
        def _(act):
            act.wait_ge(s_leakyb, 1)
            nc.scalar.activation(csq[:, :], cst[:, 0, :], ACT.Square, accum_out=cn[:, 0:1]).then_inc(s_csq, 1)
            act.wait_ge(s_csq, 1)
            nc.scalar.activation(cn[:, 1:2], cn[:, 0:1], ACT.Sqrt).then_inc(s_csq, 1)

            def dense_std(i, off):
                c, slot = NX * i + off, off % NX
                pc, rc = parts(c)
                act.wait_ge(s_var, c + 1)
                nc.scalar.activation(std[0:pc, slot, 0:rc], mv[0:pc, slot, 0:rc, 1], ACT.Sqrt,
                                     bias=eps[0:pc, :]).then_inc(s_std, 1)

            def dense_norm(i, off):
                c, slot = NX * i + off, off % NX
                pc, rc = parts(c)
                act.wait_ge(s_rstd, c + 1)
                for r in range(rc):
                    xc = added(off, r, pc) if r < by_pe(off) else xy[0:pc, slot, r, :]
                    last = nc.scalar.activation(xy[0:pc, slot, r, :], xc, ACT.Identity,
                                                scale=rstd[0:pc, slot, r:r + 1], bias=nmr[0:pc, slot, r:r + 1])
                last.then_inc(s_normed, 1)

            def dense_step(i, off, c):
                if c is None or 1 <= c:
                    dense_norm(i, off - 1)
                if c == LS:
                    act.wait_ge(s_clip, 1)
                    nc.scalar.activation(root[:, :, :], root[:, :, :], ACT.Sqrt).then_inc(s_root, 1)
                    act.wait_ge(s_root, 1)
                    for m in range(2):
                        act.dma_start(table[m * P * HI:(m + 1) * P * HI, :].rearrange("(l h) o -> l (h o)", h=HI),
                                      root[:, m, :]).then_inc(s_table, 16)
                if c is None or c < STEPS:
                    dense_std(i, off)

            dense_steps(act, dense_step)

            def carry(i, off):
                t, ring = 2 * EP * i + off, off % 2
                act.wait_ge(s_sum, t + 1)
                act.wait_ge(s_rowsin[(off + 1) % 4], 32 * (lap(2 * EP, 4, i, off + 1) + 1))
                nc.scalar.activation(xs[0:1, bass.ds((t + 1) % K, 1), :].rearrange("p o d -> p (o d)"),
                                     ps_s[off // 2 % 2][0:1, ring * D:(ring + 1) * D], ACT.Copy).then_inc(s_carry, 1)

            def operands(i, off):
                t = 2 * EP * i + off
                act.wait_ge(s_abt_ps, t + 1)
                if past(i, off, 2):
                    act.wait_ge(s_emb, t - 1)
                nc.scalar.activation(abt[:, off % 2, :, :, :].rearrange("p m k e -> p (m k e)"), ps_x[off % 2][:, :],
                                     ACT.Copy).then_inc(s_abt, 1)

            def norms(i, off):
                q, slot = EP * i + off, off % 4
                act.wait_ge(s_leaky, q + 1)
                for h in range(2):
                    if h == 1:
                        act.wait_ge(s_sq, 2 * q + 1)
                    nc.scalar.activation(sq[:, :], z[:, off % 2, h, :], ACT.Square,
                                         accum_out=ss[:, slot, h:h + 1]).then_inc(s_sq, 1)
                act.wait_ge(s_sq, 2 * q + 2)
                nc.scalar.activation(nrm[:, slot, :], ss[:, slot, :], ACT.Sqrt).then_inc(s_norm, 1)

            def edge_std(i, off):
                q, slot = EP * i + off, off % 4
                act.wait_ge(s_evar, q + 1)
                nc.scalar.activation(esd[:, slot, :], emv[:, slot, :, 1], ACT.Sqrt, bias=eps[:, :]).then_inc(s_esd, 1)

            def edge_norm(i, off):
                q, slot = EP * i + off, off % 4
                act.wait_ge(s_enm, q + 1)
                for h in range(2):
                    last = nc.scalar.activation(y[:, slot, h, :], y[:, slot, h, :], ACT.Identity,
                                                scale=ers[:, slot, h:h + 1], bias=enm[:, slot, h:h + 1])
                last.then_inc(s_done, 1)

            def pair_step(i, off, q):
                if runs(q, 0):
                    carry(i, 2 * off)
                if runs(q, 2):
                    operands(i, 2 * (off - 2) + 1)
                if runs(q, 5):
                    edge_std(i, off - 5)
                if runs(q, 6):
                    edge_norm(i, off - 6)
                if runs(q, 0) and (q is None or q < PAIRS - 1):
                    carry(i, 2 * off + 1)
                if runs(q, 1):
                    operands(i, 2 * (off - 1))
                if runs(q, 3):
                    norms(i, off - 3)

            tail_steps(dense_step, pair_step, STEPS)
            pair_steps(act, pair_step, PAIRS + 6)

        @block.vector
        def _(dve):
            done = [0]

            def setup(ins):
                done[0] += 1
                ins.then_inc(s_setup, 1)
                dve.wait_ge(s_setup, done[0])

            dve.wait_ge(s_bias, 16)
            nc.vector.scalar_tensor_tensor(out=cst[:, 0, :], in0=bb[:, 0, :], scalar=SLOPE, in1=bb[:, 0, :],
                                           op0=ALU.mult, op1=ALU.max).then_inc(s_leakyb, 1)
            dve.wait_ge(s_leakyb, 1)
            dve.wait_ge(s_iota, 1)
            setup(nc.vector.tensor_copy(iota_h[:, :], iota_i[:, :]))
            dve.wait_ge(s_csq, 2)
            setup(nc.vector.tensor_scalar(cn[:, 2:3], cn[:, 1:2], 1e-12, None, ALU.max))
            setup(nc.vector.reciprocal(cn[:, 3:4], cn[:, 2:3]))
            setup(nc.vector.tensor_scalar(cst[:, 0, :], cst[:, 0, :], cn[:, 3:4], None, ALU.mult))
            setup(nc.vector.tensor_copy(split_h[:, 0, :], cst[0:1, 0, :]))
            setup(nc.vector.tensor_tensor(split_f[:, 0, :], cst[0:1, 0, :], split_h[:, 0, :], ALU.subtract))
            setup(nc.vector.tensor_copy(split_h[:, 1, :], split_f[:, 0, :]))
            setup(nc.vector.tensor_tensor(split_f[:, 1, :], split_f[:, 0, :], split_h[:, 1, :], ALU.subtract))
            nc.vector.tensor_copy(split_h[:, 2, :], split_f[:, 1, :]).then_inc(s_split, 1)
            dve.wait_ge(s_rows, 12 * 16)
            nc.vector.tensor_copy(rows_f[:, :, :, :], rows_i[:, :, :, :]).then_inc(s_rows_f, 1)
            dve.wait_ge(s_rows_f, 1)
            setup(nc.vector.tensor_copy(rows_k[:, :, 1:P], rows_f[:, 1, :, 1:P]))
            nc.vector.tensor_copy(rows_k[:, :, 0:1], rows_f[:, 1, :, P - 1:P]).then_inc(s_rows_f, 1)
            dve.wait_ge(s_cols, 6)
            setup(nc.vector.tensor_copy(cols[:, 0:2, :].rearrange("p k t -> p (k t)"), ps[6][:, 0:2 * TILES]))
            setup(nc.vector.tensor_copy(cols[:, 2, :], ps[7][:, 0:TILES]))
            setup(nc.vector.memset(cols[0:1, 0, :], float(PAD_SRC)))
            setup(nc.vector.tensor_copy(cols_i[:, :, :], cols[:, 0:2, :]))
            setup(nc.vector.tensor_scalar(hilo_i[:, 0, :, :], cols_i[:, :, :], LO - 1, None, ALU.bitwise_and))
            setup(nc.vector.tensor_scalar(hilo_i[:, 1, :, :], cols_i[:, :, :], LO.bit_length() - 1, None, ALU.logical_shift_right))
            setup(nc.vector.tensor_copy(hilo[:, :, :, :], hilo_i[:, :, :, :]))
            setup(nc.vector.tensor_tensor(same[:, :], cols[:, 1, :], cols[:, 2, :], ALU.is_equal))
            setup(nc.vector.memset(same[0:1, :], 1.0))
            nc.vector.tensor_copy(rix[:, 0:TILES, 0], cols[:, 0, :])
            setup(nc.vector.scalar_tensor_tensor(out=rix[:, 0:TILES, 1], in0=same[:, :], scalar=float(SKIP),
                                                 in1=cols[:, 1, :], op0=ALU.mult, op1=ALU.add))
            nc.vector.tensor_copy(gix[:, :, :], rix[:, 0:K, :]).then_inc(s_gix, KP)

            def table_indices():
                for k in range(2):
                    last = nc.vector.scalar_tensor_tensor(out=tix[:, :, k], in0=hilo[:, 0, k, :], scalar=float(HI),
                                                          in1=hilo[:, 1, k, :], op0=ALU.mult, op1=ALU.add)
                setup(last)
                setup(nc.vector.memset(tix[0:1, :, :], SKIP))

            dve.wait_ge(s_cb3, 48)
            dve.wait_ge(s_keys, 32)

            def one_hots(i, off, k):
                c = NX * i + off
                t = HT * c + k
                if past(i, off, 1):
                    dve.wait_ge(s_hist, t - HT + 1)
                nc.vector.tensor_scalar(oh_lo[:, k, :], iota_h[:, 0:LO], hilo[:, 0, 0, bass.ds(t, 1)], None,
                                        ALU.is_equal)
                nc.vector.tensor_scalar(oh_hi[:, k, :], iota_h[:, :], hilo[:, 1, 0, bass.ds(t, 1)], None,
                                        ALU.is_equal).then_inc(s_onehot, 1)

            def look_up_indices(i, off):
                g, slot = NX * i + off, off % NX
                nc.vector.tensor_copy(lk_ix[:, slot, :, :], tix[:, bass.ds(g * LK, LK), :]).then_inc(s_lkix, 1)

            def edge_weight(i, off):
                g, slot = NX * i + off, off % NX
                dve.wait_ge(s_lk[slot], 32 * LK * (lap(NX, NX, i, off) + 1))
                nc.vector.tensor_tensor(lk_p[:, :], lk_v[:, slot, :, 0], lk_v[:, slot, :, 1], ALU.mult).then_inc(s_lkp, 1)
                return g

            def edge_weight_end(g):
                dve.wait_ge(s_lkp, g + 1)
                nc.vector.reciprocal(weight[:, bass.ds(g * LK, LK)], lk_p[:, :]).then_inc(s_weight, 1)

            def dense_step(i, off, c):
                n, slot = NX * i + off, off % NX
                pc, rc = parts(n)
                counting = c is None and off < LA or c is not None and c < HSTEPS
                if c is None or c < STEPS:
                    dve.wait_ge(s_load[slot], 16 * (lap(NX, NX, i, off) + 1))
                    rows = xy[0:pc, slot, by_pe(off):rc, :]
                    nc.vector.tensor_tensor(rows, rows, cst[0:pc, :, :].to_broadcast([pc, rc - by_pe(off), D]),
                                            ALU.add).then_inc(s_added, 1)
                if c is None or 1 <= c <= STEPS:
                    before = (off - 1) % NX
                    pb_, rb = parts(n - 1)
                    dve.wait_ge(s_std, n)
                    nc.vector.reciprocal(rstd[0:pb_, before, 0:rb], std[0:pb_, before, 0:rb]).then_inc(s_recip, 1)
                if counting:
                    one_hots(i, off, 0)
                if c is None or 1 <= c <= STEPS:
                    dve.wait_ge(s_recip, n)
                    nc.vector.scalar_tensor_tensor(
                        out=nmr[0:pb_, before, 0:rb], in0=mv[0:pb_, before, 0:rb, 0], scalar=-1.0,
                        in1=rstd[0:pb_, before, 0:rb], op0=ALU.mult, op1=ALU.mult).then_inc(s_rstd, 1)
                if counting:
                    for k in range(1, HT - 1):
                        one_hots(i, off, k)
                if c == HSTEPS:
                    one_hots(0, c, 0)
                if c == LS:
                    dve.wait_ge(s_hist, USED)
                    nc.vector.tensor_scalar(root[:, 0, :], hist[0][:, 0:HI], 1.0, None, ALU.max)
                    nc.vector.tensor_scalar(root[:, 1, :], hist[1][:, 0:HI], 1.0, None, ALU.max).then_inc(s_clip, 1)
                    table_indices()
                weigh = c is None and off >= LA or c is not None and LW <= c < LW + GROUPS
                if weigh:
                    g = edge_weight(i, off - LW)
                if c is None or c < STEPS:
                    dve.wait_ge(s_added, n + 1)
                    for r in range(by_pe(off), rc):
                        nc.vector.bn_stats(bst[0:pc, off % 2, r, :], xy[0:pc, slot, r, :])
                    dve.wait_ge(s_added_pe, n + 1)
                    for r in range(by_pe(off)):
                        last = nc.vector.bn_stats(bst[0:pc, off % 2, r, :], added(off, r, pc))
                    last.then_inc(s_bst, 1)
                if weigh:
                    edge_weight_end(g)
                if c is None or c < STEPS:
                    dve.wait_ge(s_bst, n + 1)
                if counting:
                    one_hots(i, off, HT - 1)
                if c is None and off >= LA or c is not None and LS <= c < LS + GROUPS:
                    look_up_indices(i, off - LS)
                if c is None or c < STEPS:
                    for r in range(rc):
                        last = nc.vector.bn_aggr(mv[0:pc, slot, r, :], bst[0:pc, off % 2, r, :])
                    last.then_inc(s_var, 1)

            dense_steps(dve, dense_step)

            def match_keys(i, off):
                q, slot = EP * i + off, off % 2
                dve.wait_ge(s_kr[off % 4], 16 * (lap(EP, 4, i, off) + 1))
                if past(i, off, 2):
                    dve.wait_ge(s_sum, 2 * q - 2)
                for h in range(2):
                    last = nc.vector.tensor_scalar(
                        match[:, slot, h, :], kr[:, off % 4, h, :], cols[:, 1, bass.ds(2 * q + h, 1)],
                        weight[:, bass.ds(2 * q + h, 1)], ALU.is_equal, ALU.mult)
                last.then_inc(s_match, 1)

            def combine(i, off, carried):
                q, slot = EP * i + off, off % 2
                dve.wait_ge(s_sum, 2 * q + 2)
                dve.wait_ge(s_carry, carried)
                if past(i, off, 2):
                    dve.wait_ge(s_abt_ps, 2 * q - 2)
                sums = ps_s[slot][:, :].rearrange("p (h d) -> p h d", h=2)
                xds = xd[:, bass.ds((2 * q) % K, 2), :]
                nc.vector.tensor_tensor(ab[:, slot, 0, :, :], sums, xds, ALU.add)
                nc.vector.tensor_tensor(ab[:, slot, 1, :, :], sums, xds, ALU.mult).then_inc(s_ab, 1)

            def add_bias(i, off):
                q, slot = EP * i + off, off % 2
                dve.wait_ge(s_emb, 2 * q + 2)
                nc.vector.tensor_tensor(z[:, slot, :, :], ps_e[slot][:, :].rearrange("p (h d) -> p h d", h=2),
                                        bb[:, :, :].to_broadcast([P, 2, D]), ALU.add).then_inc(s_z, 1)

            def leaky(i, off):
                q, slot = EP * i + off, off % 2
                dve.wait_ge(s_z, q + 1)
                nc.vector.scalar_tensor_tensor(
                    out=z[:, slot, :, :].rearrange("p h d -> p (h d)"), in0=z[:, slot, :, :].rearrange("p h d -> p (h d)"),
                    scalar=SLOPE, in1=z[:, slot, :, :].rearrange("p h d -> p (h d)"), op0=ALU.mult,
                    op1=ALU.max).then_inc(s_leaky, 1)

            def pair_step(i, off, q):
                n = EP * i + off
                slot4, slot6 = (off - 4) % 4, (off - 6) % 4
                m = n - 4
                if runs(q, 4):
                    dve.wait_ge(s_norm, m + 1)
                    nc.vector.tensor_scalar(nrc[:, slot4, :], nrm[:, slot4, :], 1e-12, None, ALU.max).then_inc(s_clamp, 1)
                if runs(q, 6):
                    dve.wait_ge(s_esd, n - 5)
                    nc.vector.reciprocal(ers[:, slot6, :], esd[:, slot6, :]).then_inc(s_ers, 1)
                if runs(q, 4):
                    dve.wait_ge(s_clamp, m + 1)
                    nc.vector.reciprocal(unit[:, slot4, :], nrc[:, slot4, :]).then_inc(s_unit, 1)
                if runs(q, 6):
                    dve.wait_ge(s_ers, n - 5)
                    nc.vector.scalar_tensor_tensor(
                        out=enm[:, slot6, :], in0=emv[:, slot6, :, 0], scalar=-1.0, in1=ers[:, slot6, :],
                        op0=ALU.mult, op1=ALU.mult).then_inc(s_enm, 1)
                if runs(q, -1):
                    match_keys(i, off + 1)
                if runs(q, 3):
                    add_bias(i, off - 3)
                if runs(q, 4):
                    if past(i, off, 8):
                        dve.wait_ge(s_scat[slot4], 32 * lap(EP, 4, i, off - 4))
                    nc.vector.tensor_copy(six[:, slot4, :, :], rix[:, bass.ds(2 * m, 2), 1:2])
                    dve.wait_ge(s_unit, m + 1)
                    for h in range(2):
                        last = nc.vector.scalar_tensor_tensor(
                            out=y[:, slot4, h, :], in0=z[:, off % 2, h, :], scalar=unit[:, slot4, h:h + 1],
                            in1=xd[:, bass.ds((2 * m + h) % K, 1), :].rearrange("p o d -> p (o d)"),
                            op0=ALU.mult, op1=ALU.add)
                    last.then_inc(s_y, 1)
                if runs(q, 3):
                    leaky(i, off - 3)
                if runs(q, 4):
                    dve.wait_ge(s_y, m + 1)
                    for h in range(2):
                        last = nc.vector.bn_stats(est[:, off % 2, h, :], y[:, slot4, h, :])
                    last.then_inc(s_est, 1)
                if runs(q, 0):
                    combine(i, off, 2 * PAIRS - 1 if q == PAIRS - 1 else 2 * n + 2)
                if runs(q, 4):
                    dve.wait_ge(s_est, m + 1)
                    if q is None or m + KP < PAIRS:
                        nc.vector.tensor_copy(gix[:, bass.ds((2 * m) % K, 2), :],
                                              rix[:, bass.ds(2 * m + K, 2), :]).then_inc(s_gix, 1)
                    for h in range(2):
                        last = nc.vector.bn_aggr(emv[:, slot4, h, :], est[:, off % 2, h, :])
                    last.then_inc(s_evar, 1)

            dve.wait_ge(s_weight, -(-2 * (EA + 1) // LK))
            match_keys(0, 0)
            tail_steps(dense_step, pair_step, STEPS)
            dve.wait_ge(s_weight, GROUPS)
            pair_steps(dve, pair_step, PAIRS + 6)

        @block.tensor
        def _(pe):
            pe.wait_ge(s_rows_f, 1)
            pe.wait_ge(s_ident, 1)
            for k in range(3):
                bank, at = (ps[6], k * TILES) if k < 2 else (ps[7], 0)
                nc.tensor.transpose(bank[:, at:at + TOP], rows_f[:, k, 0, :], ident[:, :]).then_inc(s_cols, 1)
                nc.tensor.transpose(bank[:, at + TOP:at + TILES], rows_f[0:REST, k, 1, :],
                                    ident[0:REST, 0:REST]).then_inc(s_cols, 1)

            def count_sources(i, off, k, first=False, last=False):
                t = HT * (NX * i + off) + k
                pe.wait_ge(s_onehot, t + 1)
                for m in range(2):
                    ins = nc.tensor.matmul(hist[m][:, 0:HI], oh_lo[:, k, m * P:(m + 1) * P], oh_hi[:, k, :],
                                           start=first, stop=last)
                ins.then_inc(s_hist, 1)

            def dense_step(i, off, c):
                n, slot = NX * i + off, off % NX
                pc, rc = parts(n)
                if c == 0:
                    pe.wait_ge(s_cb3, 48)
                if c is None or c < STEPS:
                    pe.wait_ge(s_load[slot], 16 * (lap(NX, NX, i, off) + 1))
                    if HSTEPS + 2 <= off < TAIL:
                        pe.wait_ge(s_normed, n - 2)
                    elif past(i, off, 2):
                        pe.wait_ge(s_normed, n - 1)
                    for r in range(by_pe(off)):
                        acc = added(off, r, pc)
                        nc.tensor.matmul(acc, ident[0:pc, 0:pc], xy[0:pc, slot, r, :], start=True, stop=False)
                        last = nc.tensor.matmul(acc, ones3[:, 0:pc], cb3[:, :], start=False, stop=True)
                    last.then_inc(s_added_pe, 1)
                if c is None and off < LA or c is not None and c < HSTEPS:
                    for k in range(HT):
                        count_sources(i, off, k, first=(c == 0 and k == 0))
                if c == HSTEPS:
                    count_sources(0, c, 0, last=True)

            dense_steps(pe, dense_step)

            def sum_edges(i, off):
                t, slot, half = 2 * EP * i + off, off // 2 % 2, off % 2
                if half == 0:
                    pe.wait_ge(s_match, EP * i + off // 2 + 1)
                    if past(i, off, 4):
                        pe.wait_ge(s_ab, EP * i + off // 2 - 1)
                pe.wait_ge(s_rowsin[off % 4], 32 * (lap(2 * EP, 4, i, off) + 1))
                if past(i, off, 1):
                    pe.wait_ge(s_carry, t)
                nc.tensor.matmul(ps_s[slot][:, half * D:(half + 1) * D], match[:, slot, half, :],
                                 xs[:, bass.ds(t % K, 1), :].rearrange("p o d -> p (o d)"), start=True,
                                 stop=True).then_inc(s_sum, 1)

            def transposes(i, off):
                t, slot, half = 2 * EP * i + off, off // 2 % 2, off % 2
                if off == 0:
                    pe.wait_ge(s_normed, TAIL)
                if half == 0:
                    pe.wait_ge(s_ab, EP * i + off // 2 + 1)
                if past(i, off, 2):
                    pe.wait_ge(s_abt, t - 1)
                for m in range(2):
                    for k in range(KB):
                        at = (m * KB + k) * P
                        last = nc.tensor.transpose(ps_x[half][:, at:at + P], ab[:, slot, m, half, k * P:(k + 1) * P],
                                                   ident[:, :])
                last.then_inc(s_abt_ps, 1)

            def products(i, off):
                t, slot, half = 2 * EP * i + off, off // 2 % 2, off % 2
                if off == 0:
                    pe.wait_ge(s_normed, TAIL)
                pe.wait_ge(s_abt, t + 1)
                if half == 0 and past(i, off, 4):
                    pe.wait_ge(s_z, EP * i + off // 2 - 1)
                acc = ps_e[slot][:, half * D:(half + 1) * D]
                for m in range(2):
                    for k in range(KB):
                        last = nc.tensor.matmul(acc, abt[:, half, m, k, :], w_sb[:, m, k, :],
                                                start=(m == 0 and k == 0), stop=(m == 1 and k == KB - 1))
                last.then_inc(s_emb, 1)

            def pair_step(i, off, q):
                if runs(q, 0):
                    sum_edges(i, 2 * off)
                if runs(q, 2):
                    transposes(i, 2 * (off - 2) + 1)
                    products(i, 2 * (off - 2))
                if runs(q, 0):
                    sum_edges(i, 2 * off + 1)
                if runs(q, 1):
                    transposes(i, 2 * (off - 1))
                if runs(q, 2):
                    products(i, 2 * (off - 2) + 1)

            pe.wait_ge(s_w, 32)
            pe.wait_ge(s_zero, 2)
            pe.wait_ge(s_clip, 1)
            tail_steps(dense_step, pair_step, STEPS - 1)
            pair_steps(pe, pair_step, PAIRS + 2)


_INS = ['x', 'src', 'dst', 'L0_gnn_W1', 'L0_gnn_W2', 'L0_gnn_b']
_OUTS = [((100000, 256), 'float32')]


def kernel(**inputs):
    import numpy as _np
    import concourse.bacc as _bacc
    from concourse import mybir as _mybir
    from concourse.bass_utils import run_bass_kernel_spmd as _run

    nc = _bacc.Bacc("TRN2", target_bir_lowering=False, num_devices=1)
    arrays, args = {}, []
    for name in _INS:
        a = _np.ascontiguousarray(inputs[name])
        arrays[f"in_{name}_dram"] = a
        args.append(nc.dram_tensor(f"in_{name}_dram", a.shape, _mybir.dt.from_np(a.dtype), kind="ExternalInput").ap())
    for i, (shape, dtype) in enumerate(_OUTS):
        dt = _mybir.dt.from_np(_np.dtype(dtype))
        args.append(nc.dram_tensor(f"out_{i}_dram", shape, dt, kind="ExternalOutput").ap())
    gnn_resnorm(nc, *args)
    r = _run(nc, [arrays], core_ids=[0])
    got = tuple(r.results[0][f"out_{i}_dram"] for i in range(len(_OUTS)))
    return got[0]
```
